# Optimizing a Trainium2 kernel written in Bass

```python
import numpy as np
import jax
import jax.numpy as jnp

def _softmax(x, axis=-1):
    return jax.nn.softmax(x, axis=axis)

def _gelu(x):
    return jax.nn.gelu(x, approximate=True)

def _silu(x):
    return jax.nn.silu(x)

def _sigmoid(x):
    return jax.nn.sigmoid(x)

def _layernorm(x, axis=-1, eps=1e-05):
    m = jnp.mean(x, axis=axis, keepdims=True)
    v = jnp.var(x, axis=axis, keepdims=True)
    return (x - m) / jnp.sqrt(v + eps)

def _scatter_add(tgt, idx, src, axis=0):
    return tgt.at[idx].add(src)

def _segment_sum(src, seg, n):
    return jax.ops.segment_sum(src, seg, n)
kernel_name = 'mk_xattn_ffn_d1_seqx_r4_076a68'

def setup_inputs(seed: int=0):
    np.random.seed(seed)
    _w = jnp.asarray

    def _rec_inputs():
        import jax
        import jax.numpy as jnp
        _rk = jax.random.key(seed)
        x = -0.0005207 + 1.001 * jax.random.normal(jax.random.fold_in(_rk, 1), (4, 512, 1024), jnp.float32)
        _lenS = 512 - jax.random.randint(jax.random.fold_in(_rk, 7), (4,), 0, max(1, 512 // 4) + 1, jnp.int32)
        _lenS2 = 64 - jax.random.randint(jax.random.fold_in(_rk, 8), (4,), 0, max(1, 64 // 4) + 1, jnp.int32)
        _ctx_4096P = jax.random.normal(jax.random.fold_in(_rk, 11), (4, 16, 1024), jnp.float32)
        _ctx_4096c = jax.random.dirichlet(jax.random.fold_in(_rk, 511), 0.3 * jnp.ones((16,), jnp.float32), (4, 64))
        _ctx_4096t = jnp.einsum('bsk,bkd->bsd', _ctx_4096c, _ctx_4096P)
        _ctx_4096t = _ctx_4096t * jax.lax.rsqrt(jnp.mean(jnp.square(_ctx_4096t)) + 1e-12) * 0.953939
        ctx_4096 = -0.00010331 + 0.999899 * (_ctx_4096t + 0.3 * jax.random.normal(jax.random.fold_in(_rk, 611), (4, 64, 1024), jnp.float32))
        return (x, ctx_4096)
    x, ctx_4096 = _rec_inputs()

    def _L0_xattn_setup():
        import jax, jax.numpy as jnp
        import numpy as np
        B, Q, D = (8, 64, 1024)
        CTX = 1024
        H, KV, HD = (16, 4, 96)
        G = H // KV
        key = jax.random.key(seed)
        ks = jax.random.split(key, 6)
        s = 0.02
        return {'latents': jax.random.normal(ks[0], (B, Q, D), jnp.float32), 'context': jax.random.normal(ks[1], (B, CTX, D), jnp.float32), 'Wq': jax.random.normal(ks[2], (H * HD, D), jnp.float32) * s, 'Wk': jax.random.normal(ks[3], (KV * HD, D), jnp.float32) * s, 'Wv': jax.random.normal(ks[4], (KV * HD, D), jnp.float32) * s, 'Wo': jax.random.normal(ks[5], (D, H * HD), jnp.float32) * s}
    _L0_xattn_all = _L0_xattn_setup()
    _L0_xattn_in = {k: v for k, v in _L0_xattn_all.items() if k in ('Wq', 'Wk', 'Wv', 'Wo')}
    del _L0_xattn_all

    def _L0_ffn_setup():
        import jax, jax.numpy as jnp
        import numpy as np
        HID, INT, LAT, NE, K = (1024, 2048, 512, 8, 2)
        LN_EPS = 1e-05

        def _layernorm(x, gamma, beta):
            mu = jnp.mean(x, axis=-1, keepdims=True)
            var = jnp.var(x, axis=-1, keepdims=True)
            return (x - mu) * jax.lax.rsqrt(var + LN_EPS) * gamma + beta
        key = jax.random.key(seed)
        ks = jax.random.split(key, 8)
        s = lambda d: 1.0 / np.sqrt(d)
        return {'hidden_states': jax.random.normal(ks[0], (4, 512, HID), jnp.float32), 'gate_w': jax.random.normal(ks[1], (HID, NE), jnp.float32) * s(HID), 'up_w': jax.random.normal(ks[2], (HID, INT), jnp.float32) * s(HID), 'down_w': jax.random.normal(ks[3], (INT, HID), jnp.float32) * s(INT), 'fc1_w': jax.random.normal(ks[4], (HID, LAT), jnp.float32) * s(HID), 'fc2_w': jax.random.normal(ks[5], (LAT, HID), jnp.float32) * s(LAT), 'expert_w': jax.random.normal(ks[6], (LAT, LAT), jnp.float32), 'ln_gamma': jnp.ones((HID,), jnp.float32), 'ln_beta': jnp.zeros((HID,), jnp.float32)}
    _L0_ffn_all = _L0_ffn_setup()
    _L0_ffn_in = {k: v for k, v in _L0_ffn_all.items() if k in ('gate_w', 'up_w', 'down_w', 'fc1_w', 'fc2_w', 'expert_w', 'ln_gamma', 'ln_beta')}
    del _L0_ffn_all
    return {'x': x, 'ctx_4096': ctx_4096, 'L0_xattn_Wq': _L0_xattn_in['Wq'], 'L0_xattn_Wk': _L0_xattn_in['Wk'], 'L0_xattn_Wv': _L0_xattn_in['Wv'], 'L0_xattn_Wo': _L0_xattn_in['Wo'], 'L0_ffn_gate_w': _L0_ffn_in['gate_w'], 'L0_ffn_up_w': _L0_ffn_in['up_w'], 'L0_ffn_down_w': _L0_ffn_in['down_w'], 'L0_ffn_fc1_w': _L0_ffn_in['fc1_w'], 'L0_ffn_fc2_w': _L0_ffn_in['fc2_w'], 'L0_ffn_expert_w': _L0_ffn_in['expert_w'], 'L0_ffn_ln_gamma': _L0_ffn_in['ln_gamma'], 'L0_ffn_ln_beta': _L0_ffn_in['ln_beta']}

def reference(x, ctx_4096, L0_xattn_Wq, L0_xattn_Wk, L0_xattn_Wv, L0_xattn_Wo, L0_ffn_gate_w, L0_ffn_up_w, L0_ffn_down_w, L0_ffn_fc1_w, L0_ffn_fc2_w, L0_ffn_expert_w, L0_ffn_ln_gamma, L0_ffn_ln_beta):
    import jax
    import jax.numpy as jnp

    def _L0_xattn_ref(latents, context, Wq, Wk, Wv, Wo):
        import jax, jax.numpy as jnp
        import numpy as np
        B, Q, D = (8, 64, 1024)
        CTX = 1024
        H, KV, HD = (16, 4, 96)
        G = H // KV
        b, q_len, _ = latents.shape
        hidden = jnp.concatenate([context, latents], axis=1)
        s_len = hidden.shape[1]
        q = (latents @ Wq.T).reshape(b, q_len, H, HD)
        k = (hidden @ Wk.T).reshape(b, s_len, KV, HD)
        v = (hidden @ Wv.T).reshape(b, s_len, KV, HD)
        q = q.transpose(0, 2, 1, 3).reshape(b, KV, G, q_len, HD)
        k = k.transpose(0, 2, 1, 3)
        v = v.transpose(0, 2, 1, 3)
        scale = 1.0 / jnp.sqrt(jnp.asarray(HD, q.dtype))
        scores = jnp.einsum('bkgqd,bksd->bkgqs', q, k) * scale
        attn = jax.nn.softmax(scores.astype(jnp.float32), axis=-1).astype(q.dtype)
        out = jnp.einsum('bkgqs,bksd->bkgqd', attn, v)
        out = out.reshape(b, H, q_len, HD).transpose(0, 2, 1, 3).reshape(b, q_len, H * HD)
        return out @ Wo.T

    def _L0_ffn_ref(hidden_states, gate_w, up_w, down_w, fc1_w, fc2_w, expert_w, ln_gamma, ln_beta):
        import jax, jax.numpy as jnp
        import numpy as np
        HID, INT, LAT, NE, K = (1024, 2048, 512, 8, 2)
        LN_EPS = 1e-05

        def _layernorm(x, gamma, beta):
            mu = jnp.mean(x, axis=-1, keepdims=True)
            var = jnp.var(x, axis=-1, keepdims=True)
            return (x - mu) * jax.lax.rsqrt(var + LN_EPS) * gamma + beta
        logits = jnp.einsum('bsh,he->bse', hidden_states, gate_w)
        routing_weights, selected_experts = jax.lax.top_k(logits, K)
        h = jax.nn.relu(jnp.einsum('bsh,hi->bsi', hidden_states, up_w)) ** 2
        shared_out = jnp.einsum('bsi,ih->bsh', h, down_w)
        x_latent = jnp.einsum('bsh,hl->bsl', hidden_states, fc1_w)
        expert_out = jnp.einsum('bsl,lm->bsm', x_latent, expert_w)
        moe_out = expert_out * jnp.sum(routing_weights, axis=-1, keepdims=True)
        routed_out = jnp.einsum('bsl,lh->bsh', moe_out, fc2_w)
        return _layernorm(shared_out + routed_out, ln_gamma, ln_beta)
    x = x + _L0_xattn_ref(_layernorm(x, axis=-1), ctx_4096, L0_xattn_Wq, L0_xattn_Wk, L0_xattn_Wv, L0_xattn_Wo)
    x = x + _L0_ffn_ref(_layernorm(x, axis=-1), L0_ffn_gate_w, L0_ffn_up_w, L0_ffn_down_w, L0_ffn_fc1_w, L0_ffn_fc2_w, L0_ffn_expert_w, L0_ffn_ln_gamma, L0_ffn_ln_beta)
    return x

_drawn_inputs = setup_inputs


def setup_inputs(seed=0):
    import zlib

    import numpy as np

    out = dict(_drawn_inputs(seed))
    spreads = {'L0_ffn_ln_gamma': (1.0, 0.2), 'L0_ffn_ln_beta': (0.0, 0.1)}
    factors = {'L0_xattn_Wq': 3.514, 'L0_xattn_Wk': 3.568}
    for name, (base, spread) in spreads.items():
        noise = np.random.default_rng([zlib.crc32(name.encode()), seed]).standard_normal(out[name].shape)
        drawn = base * np.exp(spread * noise) if base else spread * noise
        out[name] = jnp.asarray(drawn.astype(out[name].dtype))
    for name, factor in factors.items():
        out[name] = (out[name] * factor).astype(out[name].dtype)
    return out
```

```python
import concourse.bass as bass
from concourse import mybir
from contextlib import ExitStack


def xattn_ffn_kernel(nc, x, ctx, wqkv, wo, gate_w, up_w, down_w, fc1_w, fc2_w, expert_w, gamma, beta, out):
    f32 = mybir.dt.float32
    f32r = mybir.dt.float32r
    ALU = mybir.AluOpType
    ACT = mybir.ActivationFunctionType
    AX = mybir.AxisListType

    P = 128
    B, S, D = x.shape
    C = ctx.shape[1]
    T = S + C
    HD = 96
    E = wo.shape[1]
    H = E // HD
    KVE = (wqkv.shape[0] - E) // 2
    KV = KVE // HD
    G = H // KV
    F = up_w.shape[1]
    L = fc1_w.shape[1]
    NE = gate_w.shape[1]
    EPS = 1e-5
    SCALE = float(HD) ** -0.5

    DK = D // P
    ST = S // P
    NT = T // P + 1
    QC, KC = E // P, KVE // P
    FC, LC = F // P, L // P
    NB = S
    assert D == 1024 and S == 512 and C == 64 and NT == 5 and KC == 3 and QC == 12 and G == 4

    def dram(name, shape):
        return nc.dram_tensor(name, shape, f32, kind="Internal").ap()

    q_d = dram("q_scratch", (B * E, S))
    k_d = dram("k_scratch", (B * KVE, T))
    v_d = dram("v_scratch", (B * KV * T, HD))
    o_d = dram("o_scratch", (B * E, S))
    x1_d = dram("x1_scratch", (B * S, D))
    h_d = dram("h_scratch", (B * (F + L), S))
    w_d = dram("fold_scratch", (L, D))

    x_r = x.rearrange("b s d -> (b s) d")
    out_r = out.rearrange("b s d -> (b s) d")

    es = ExitStack()
    with es:
        SLOT = 2 * D
        MM = es.enter_context(nc.sbuf_tensor("operands", [P, 22 * SLOT + 1024], f32r))
        SF = es.enter_context(nc.sbuf_tensor("staging", [P, 6656], f32))
        ident = es.enter_context(nc.sbuf_tensor("ident", [P, P], f32))
        sm = es.enter_context(nc.sbuf_tensor("small", [P, 320], f32))
        PS = es.enter_context(nc.psum_tensor("psum", [P, 8, NB], f32))

        def mmf(a, n, p=P, p0=0):
            return MM[p0:p0 + p, a:a + n]

        def raw(ap):
            return ap.bitcast(f32)

        def slot_hi(s):
            return mmf(s * SLOT, D)

        def slot_lo(s):
            return mmf(s * SLOT + D, D)

        Z0 = 18 * SLOT
        zhi = mmf(Z0, DK * S).rearrange("p (k s) -> p k s", k=DK)
        zlo = mmf(Z0 + DK * S, DK * S).rearrange("p (k s) -> p k s", k=DK)

        GW = mmf(22 * SLOT, DK * 2 * NE).rearrange("p (k e) -> p k e", k=DK)

        stats = sm[:, 0:48].rearrange("p (t h s) -> p t h s", t=4, h=2)
        mv = sm[:, 48:56].rearrange("p (t s) -> p t s", t=4)
        ve, rec, rt, nt1, rstd = (sm[:, 56 + 4 * i:60 + 4 * i] for i in range(5))
        negmax = sm[:, 80:88]
        gsum = sm[:, 88:152].rearrange("p (t e) -> p t e", t=4)
        g8 = sm[:, 152:184].rearrange("p (t e) -> p t e", t=4)
        gtop = sm[:, 184:216].rearrange("p (t e) -> p t e", t=4)
        rw = sm[:, 216:232]
        rsum, rrec = sm[:, 296:304], sm[:, 304:312]
        graw = sm[:, 232:296].rearrange("p (k e) -> p k e", k=DK)

        sems = {}

        def sem(name, credit=0):
            s = es.enter_context(nc.semaphore(name))
            sems[name] = (s, credit)
            return name

        def ge(e, name, v):
            s, c = sems[name]
            e.wait_ge(s, v + c)

        def hold(e, name, v):
            ge(e, name, v)
            e.sem_inc(idle, 1)

        def inc(ins, name, n=1):
            ins.then_inc(sems[name][0], n)

        idle = es.enter_context(nc.semaphore("idle"))

        def parts3(e, o, lh, ll, rh, rl, first, last):
            e.matmul(o, lh, rh, start=first, stop=False)
            e.matmul(o, lh, rl, start=False, stop=False)
            return e.matmul(o, ll, rh, start=False, stop=last)

        ph_start = sem("constants_ready")

        def weight_prep(tag, n, src, slot0, raw_at, nb=3):
            ld = [sem(f"{tag}_raw{p}") for p in range(nb)]
            tr = sem(f"{tag}_transposed", nb)
            hi = sem(f"{tag}_hi")
            lo = sem(f"{tag}_lo", nb)
            rawb = [SF[:, raw_at + p * D:raw_at + (p + 1) * D] for p in range(nb)]
            bank = [PS[:, 2 * p:2 * p + 2, :].rearrange("p b n -> p (b n)") for p in range(nb)]
            assert n % nb == 0

            def dst(i, p, off):
                return MM[:, bass.ds(i * (nb * SLOT) + ((slot0 + p) * SLOT + off), D)]

            def sp(e):
                with e.Fori(0, n // nb) as i:
                    for p in range(nb):
                        hold(e, tr, i * nb + p + 1 - nb)
                        view = src(i * nb + p)
                        o = rawb[p] if len(view.shape) == 2 else rawb[p].rearrange("p (i e) -> p i e", e=P)
                        inc(e.dma_start(o, view), ld[p], 16)

            def pe(e):
                with e.Fori(0, n // nb) as i:
                    for p in range(nb):
                        ge(e, ld[p], i * 16 + 16)
                        ge(e, lo, i * nb + p + 1 - nb)
                        for k in range(DK):
                            m = e.transpose(bank[p][:, k * P:(k + 1) * P], rawb[p][:, k * P:(k + 1) * P], ident[:])
                        inc(m, tr)

            def act(e):
                with e.Fori(0, n // nb) as i:
                    for p in range(nb):
                        ge(e, tr, i * nb + p + 1)
                        inc(e.activation(dst(i, p, 0), bank[p], ACT.Copy), hi)

            def dve(e):
                with e.Fori(0, n // nb) as i:
                    for p in range(nb):
                        ge(e, hi, i * nb + p + 1)
                        inc(e.tensor_tensor(dst(i, p, D), bank[p], raw(dst(i, p, 0)), ALU.subtract), lo)

            return sp, pe, act, dve, lo, tr

        LN_CHAIN = 18

        def norm_z(tag, xn, last_free):
            ld = sem(f"{tag}_x")
            ch = sem(f"{tag}_chain")
            sq = sem(f"{tag}_sqrt")
            zn = sem(f"{tag}_z")
            zt = sem(f"{tag}_zt", 8)
            zh = sem(f"{tag}_zhi")
            zl = sem(f"{tag}_zlo", 8)
            fr = sem(f"{tag}_zfree", DK)

            def load(e, src, b):
                hold(e, zt, b * DK)
                inc(e.dma_start(xn, src[bass.ds(b * S, S), :].rearrange("(t p) d -> p t d", p=P)), ld, 16)

            def dve_norm(e, b):
                n = [0]

                def link(ins, last=True):
                    n[0] += 1
                    inc(ins, ch)
                    if last:
                        hold(e, ch, b * LN_CHAIN + n[0])

                hold(e, ld, b * 16 + 16)
                for t in range(ST):
                    for h in range(2):
                        link(e.bn_stats(stats[:, t, h, :], xn[:, t, h * NB:(h + 1) * NB]), (t, h) == (ST - 1, 1))
                for t in range(ST):
                    link(e.bn_aggr(mv[:, t, :], stats[:, t, :, :]), t == ST - 1)
                link(e.tensor_scalar(ve, mv[:, :, 1], EPS, None, ALU.add))
                link(e.reciprocal(rec, ve))
                hold(e, sq, b + 1)
                link(e.tensor_tensor(nt1, rt, rt, ALU.mult))
                link(e.tensor_tensor(nt1, nt1, ve, ALU.mult))
                link(e.tensor_scalar(nt1, nt1, -0.5, 1.5, ALU.mult, ALU.add))
                link(e.tensor_tensor(rstd, rt, nt1, ALU.mult))
                assert n[0] == LN_CHAIN
                for t in range(ST):
                    z = e.tensor_scalar(xn[:, t, :], xn[:, t, :], mv[:, t, 0:1], rstd[:, t:t + 1], ALU.subtract, ALU.mult)
                inc(z, zn)

            def act_sqrt(e, b):
                ge(e, ch, b * LN_CHAIN + 14)
                inc(e.activation(rt, rec, ACT.Sqrt), sq)

            def pe_t(e, b, k):
                if k == 0:
                    ge(e, zn, b + 1)
                ge(e, zl, b * DK + k - 1)
                for t in range(ST):
                    m = e.transpose(PS[:, 6 + k % 2, t * P:(t + 1) * P], xn[:, t, k * P:(k + 1) * P], ident[:])
                inc(m, zt)

            def act_hi(e, b, k):
                ge(e, zt, b * DK + k + 1)
                if k < DK - 1:
                    ge(e, fr, (b - 1) * (DK - 1) + k + 1)
                else:
                    last_free(e, b)
                inc(e.activation(zhi[:, k, :], PS[:, 6 + k % 2, :], ACT.Copy), zh)

            def dve_lo(e, b, k):
                ge(e, zh, b * DK + k + 1)
                inc(e.tensor_tensor(zlo[:, k, :], PS[:, 6 + k % 2, :], raw(zhi[:, k, :]), ALU.subtract), zl)

            return load, dve_norm, act_sqrt, pe_t, act_hi, dve_lo, zl, fr, zt

        def mm_groups(e, b, groups, lo_sem, pe_t, wait_bank, slot_of, done, slot_ready=None, after_group=None, free=None):
            for g, chunks in enumerate(groups):
                wait_bank(g)
                for k in range(DK):
                    if g == 0:
                        if k == 0:
                            pe_t(e, b, 0)
                            pe_t(e, b, 1)
                        ge(e, lo_sem, b * DK + k + 1)
                    for c, ch in enumerate(chunks):
                        if k == 0 and slot_ready:
                            slot_ready(ch)
                        s = slot_of(ch)
                        wh, wl = slot_hi(s)[:, k * P:(k + 1) * P], slot_lo(s)[:, k * P:(k + 1) * P]
                        m = parts3(e, PS[:, 3 * (g % 2) + c, :], wh, wl, zhi[:, k, :], zlo[:, k, :], k == 0, k == DK - 1)
                        if k == DK - 1:
                            inc(m, done)
                    if free and g == len(groups) - 1 and k < DK - 1:
                        inc(m, free)
                    if g == 0 and k + 2 < DK:
                        pe_t(e, b, k + 2)
                if after_group:
                    after_group(g)

        f_ld = [sem(f"fold_load{t}") for t in range(LC + 1)]
        f_t, f_xhi, f_xlo, f_hi, f_lo, f_mm, f_ev, f_st = (sem(f"fold_{n}") for n in (
            "transposed", "expert_hi", "expert_lo", "fc2_hi", "fc2_lo", "product", "staged", "stored"))
        ex_raw = SF[:, 0:LC * L].rearrange("p (t m) -> p t m", t=LC)
        f2_raw = SF[:, LC * L:LC * L + LC * D]
        exT = [mmf(i * LC * L, LC * L).rearrange("p (t l) -> p t l", t=LC) for i in range(2)]
        f2 = [mmf(2 * LC * L + i * LC * D, LC * D).rearrange("p (t n) -> p t n", t=LC) for i in range(2)]
        fold_out = f2_raw

        def fold_sp(e):
            inc(e.dma_start(ex_raw, expert_w.rearrange("(t p) m -> p t m", p=P)), f_ld[LC], 16)
            for t in range(LC):
                inc(e.dma_start(f2_raw[:, t * D:(t + 1) * D], fc2_w[t * P:(t + 1) * P, :]), f_ld[t], 16)
            ge(e, f_t, 1)

        def fold_store(e):
            ge(e, f_ev, 1)
            inc(e.dma_start(w_d.rearrange("(t p) n -> p t n", p=P), fold_out.rearrange("p (t n) -> p t n", t=LC)), f_st, 16)
            ge(e, f_st, 16)

        def fold_pe(e):
            ge(e, f_ld[LC], 16)
            ge(e, ph_start, 2)
            for mt in range(LC):
                for lt in range(LC):
                    m = e.transpose(PS[:, mt, lt * P:(lt + 1) * P], ex_raw[:, lt, mt * P:(mt + 1) * P], ident[:])
            inc(m, f_t)
            for mt in range(LC):
                if mt == 0:
                    ge(e, f_xlo, 1)
                ge(e, f_lo, mt + 1)
                for lt in range(LC):
                    for h in range(2):
                        lw = [t[:, mt, lt * P:(lt + 1) * P] for t in exT]
                        rv = [t[:, mt, h * NB:(h + 1) * NB] for t in f2]
                        m = parts3(e, PS[:, 2 * lt + h, :], lw[0], lw[1], rv[0], rv[1], mt == 0, mt == LC - 1)
            inc(m, f_mm)

        def fold_act(e):
            ge(e, f_ld[LC], 16)
            for t in range(LC + 1):
                if t == 1:
                    ge(e, f_t, 1)
                    inc(e.activation(exT[0], PS[:, 0:LC, :], ACT.Copy), f_xhi)
                c = t - 1 if t > 1 else t
                if t != 1:
                    ge(e, f_ld[c], 16)
                    inc(e.activation(f2[0][:, c, :], f2_raw[:, c * D:(c + 1) * D], ACT.Copy), f_hi)

        def fold_evac(e):
            ge(e, f_mm, 1)
            ge(e, f_lo, LC)
            inc(e.activation(fold_out, PS[:, :, :].rearrange("p b n -> p (b n)"), ACT.Copy), f_ev)

        def fold_dve(e):
            for t in range(LC):
                ge(e, f_hi, t + 1)
                inc(e.tensor_tensor(f2[1][:, t, :], f2_raw[:, t * D:(t + 1) * D], raw(f2[0][:, t, :]), ALU.subtract), f_lo)
                if t == 0:
                    ge(e, f_xhi, 1)
                    inc(e.tensor_tensor(exT[1], PS[:, 0:LC, :], raw(exT[0]), ALU.subtract), f_xlo)

        XN = SF[:, 0:ST * D].rearrange("p (t d) -> p t d", t=ST)
        wa_sp, wa_pe, wa_act, wa_dve, wa_lo, wa_tr = weight_prep(
            "wqkv", QC + 2 * KC, lambda j: wqkv[bass.ds(j * P, P), :], 0, 0)
        n_wa = QC + 2 * KC

        BC = B * C
        ctx_raw = SF[:, 4 * D:6 * D].rearrange("p (t d) -> p t d", t=2)
        cT = [mmf(Z0 + i * DK * BC, DK * BC).rearrange("p (k s) -> p k s", k=DK) for i in range(2)]
        STG = 4 * D
        stage = [SF[:, STG + c * NB:STG + (c + 1) * NB] for c in range(3)]
        vstage = [SF[:, STG + 3 * NB + t * KVE:STG + 3 * NB + (t + 1) * KVE] for t in range(2)]
        c_ld, c_t, c_hi, c_lo, c_mm, c_ev, c_st = (sem(f"ctx_{n}") for n in
                                                   ("load", "transposed", "hi", "lo", "product", "staged", "stored"))
        v_w = [MM[:, 15 * SLOT:18 * SLOT].rearrange("p (c h k e) -> p h k c e", c=KC, h=2, k=DK)[:, i] for i in range(2)]
        v_rows = v_d.rearrange("(q s) d -> q s d", s=T)
        k_b = k_d.rearrange("(b e) s -> e b s", b=B)

        def ctx_sp(e):
            inc(e.dma_start(ctx_raw, ctx.rearrange("(t b) s d -> (b s) t d", t=2)), c_ld, 16)

        def ctx_pe(e):
            ge(e, c_ld, 16)
            ge(e, wa_lo, n_wa)
            for k in range(DK):
                for t in range(2):
                    at = k * BC + t * P
                    m = e.transpose(PS[:, at // NB, at % NB:at % NB + P], ctx_raw[:, t, k * P:(k + 1) * P], ident[:])
            inc(m, c_t)
            ge(e, c_lo, 1)
            for c in range(KC):
                s = QC + c
                for k in range(DK):
                    wh, wl = slot_hi(s)[:, k * P:(k + 1) * P], slot_lo(s)[:, k * P:(k + 1) * P]
                    m = parts3(e, PS[:, 4 + c, 0:BC], wh, wl, cT[0][:, k, :], cT[1][:, k, :], k == 0, k == DK - 1)
                inc(m, c_mm)
            for t in range(2):
                for k in range(DK):
                    zt_ = [z[:, k, t * P:(t + 1) * P] for z in cT]
                    m = parts3(e, PS[:, t, 0:KVE], zt_[0], zt_[1], v_w[0][:, k], v_w[1][:, k], k == 0, k == DK - 1)
                inc(m, c_mm)

        def ctx_act(e):
            ge(e, c_t, 1)
            flat = PS[:, 0:4, :].rearrange("p b n -> p (b n)")
            inc(e.activation(mmf(Z0, DK * BC), flat, ACT.Copy), c_hi)
            a_sqrt(e, 0)
            for c in range(KC):
                ge(e, c_mm, c + 1)
                inc(e.activation(stage[c][:, 0:BC], PS[:, 4 + c, 0:BC], ACT.Copy), c_ev)
            for t in range(2):
                ge(e, c_mm, KC + t + 1)
                inc(e.activation(vstage[t], PS[:, t, 0:KVE], ACT.Copy), c_ev)
            for c in range(KC):
                ge(e, c_ev, KC + 2)
                inc(e.dma_start(k_b[c * P:(c + 1) * P, :, S:T], stage[c][:, 0:BC].rearrange("p (b s) -> p b s", b=B)), c_st, 16)
            for t in range(2):
                for h in range(2):
                    inc(e.dma_start(v_rows[(2 * t + h) * KV:(2 * t + h + 1) * KV, S:T, :].rearrange("h s d -> s h d"),
                                    vstage[t][h * C:(h + 1) * C, :].rearrange("p (h d) -> p h d", d=HD)), c_st, 16)
            ge(e, c_st, 16 * (KC + 4))

        def ctx_dve(e):
            ge(e, c_hi, 1)
            inc(e.tensor_tensor(mmf(Z0 + DK * BC, DK * BC), PS[:, 0:4, :].rearrange("p b n -> p (b n)"),
                                raw(mmf(Z0, DK * BC)), ALU.subtract), c_lo)

        a_acc = sem("a_product", 1)
        a_ev = sem("a_staged", 1)
        a_st = [sem(f"a_stored{c}", 16) for c in range(3)]
        a_vst = [sem(f"a_vstored{t}", 16) for t in range(2)]
        A_GROUPS = [[QC, QC + 1, QC + 2]] + [[3 * g, 3 * g + 1, 3 * g + 2] for g in range(QC // 3)]
        NQK = QC + KC
        A_EV = NQK + ST
        a_load, a_norm, a_sqrt, a_pet, a_hi, a_lo, a_zl, a_fr, a_zt = norm_z(
            "a", XN, lambda e, b: ge(e, a_acc, b * A_EV))

        def a_sp(e):
            hold(e, wa_tr, n_wa)
            with e.Fori(0, B) as b:
                a_load(e, x_r, b)

        def a_pe(e):
            ge(e, c_ev, KC + 2)
            with e.Fori(0, B) as b:
                def wait_bank(g):
                    ge(e, a_ev, b * A_EV + (3 * (g - 1) if g >= 2 else 0))

                mm_groups(e, b, A_GROUPS, a_zl, a_pet, wait_bank, lambda ch: ch, a_acc)
                for g in range(2):
                    ge(e, a_ev, b * A_EV + 3 * (len(A_GROUPS) - 1 + g))
                    for k in range(DK):
                        for c in range(2):
                            t = 2 * g + c
                            zt_ = [z[:, k, t * P:(t + 1) * P] for z in (zhi, zlo)]
                            m = parts3(e, PS[:, 3 * ((g + 1) % 2) + c, 0:KVE], zt_[0], zt_[1],
                                       v_w[0][:, k], v_w[1][:, k], k == 0, k == DK - 1)
                            if k == DK - 1:
                                inc(m, a_acc)
                        if g == 1 and k < DK - 1:
                            inc(m, a_fr)

        def a_act(e):
            def body(b, last):
                for k in range(DK):
                    a_hi(e, b, k)
                for g, chunks in enumerate(A_GROUPS):
                    for c, ch in enumerate(chunks):
                        n = 3 * g + c
                        ge(e, a_acc, b * A_EV + n + 1)
                        ge(e, a_st[c], b * (16 * len(A_GROUPS)) + 16 * g)
                        inc(e.activation(stage[c], PS[:, 3 * (g % 2) + c, :], ACT.Copy, scale=SCALE if ch < QC else 1.0), a_ev)
                        ge(e, a_ev, b * A_EV + n + 1)
                        if ch < QC:
                            dst = q_d[bass.ds(b * E + ch * P, P), :]
                        else:
                            dst = k_d[bass.ds(b * KVE + (ch - QC) * P, P), 0:S]
                        inc(e.dma_start(dst, stage[c]), a_st[c], 16)
                    if g == 2 and not last:
                        a_sqrt(e, b + 1)
                for t in range(ST):
                    n = NQK + t
                    g, c = t // 2, t % 2
                    ge(e, a_acc, b * A_EV + n + 1)
                    ge(e, a_vst[c], b * (16 * (ST // 2)) + 16 * g)
                    inc(e.activation(vstage[c], PS[:, 3 * ((g + 1) % 2) + c, 0:KVE], ACT.Copy), a_ev)
                    ge(e, a_ev, b * A_EV + n + 1)
                    dst = v_rows[bass.ds(b * KV, KV), t * P:(t + 1) * P, :].rearrange("h s d -> s h d")
                    inc(e.dma_start(dst, vstage[c].rearrange("p (h d) -> p h d", d=HD)), a_vst[c], 16)

            with e.Fori(0, B - 1) as b:
                body(b, False)
            body(B - 1, True)

        def a_dve(e):
            with e.Fori(0, B) as b:
                a_norm(e, b)
                for k in range(DK):
                    a_lo(e, b, k)

        def a_stored(e):
            for c in range(3):
                ge(e, a_st[c], 16 * B * len(A_GROUPS))
            for t in range(2):
                ge(e, a_vst[t], 16 * B * (ST // 2))

        WO0 = 6
        wo_v = wo.rearrange("(i p) e -> p i e", p=P)
        wb_sp, wb_pe, wb_act, wb_dve, wb_lo, wb_tr = weight_prep(
            "wo", QC, lambda j: wo_v[:, :, bass.ds(j * P, P)], WO0, 0)

        NG = B * KV
        NH = NG * G
        KB, VB, PB, QB = 0, 4 * T, 4608, Z0
        VW = HD
        kp = [[mmf(KB + p * 2 * T + i * T, T, HD) for i in range(2)] for p in range(2)]
        vp = [[mmf(VB + (2 * p + i) * NT * VW, NT * VW).rearrange("p (j d) -> p j d", j=NT) for i in range(2)] for p in range(2)]
        qp = [[mmf(QB + (2 * p + i) * G * S, G * S, HD) for i in range(2)] for p in range(2)]
        pt = [[mmf(PB + (2 * j + i) * S, S) for i in range(2)] for j in range(NT)]
        assert VB + 4 * NT * VW <= PB and PB + 2 * NT * S <= WO0 * SLOT
        pu = [[SF[:, (hp * ST + u) * T:(hp * ST + u + 1) * T] for u in range(ST)] for hp in range(2)]
        OS0 = 2 * ST * T
        os_ = [SF[0:HD, OS0 + r * S:OS0 + (r + 1) * S] for r in range(2)]
        su = [PS[:, 2 * i:2 * i + 2, :].rearrange("p b n -> p (b n)") for i in range(2)]
        TB = [4, 5, 6, 4, 5]
        b_ld = [sem(f"b_loaded{p}") for p in range(2)]
        b_sp, b_S, b_T = sem("b_split"), sem("b_scores"), sem("b_transposed", 10)
        b_mx, b_ex, b_hi, b_lo = sem("b_max"), sem("b_exp", 2), sem("b_hi"), sem("b_lo", 5)
        b_pv, b_oe = sem("b_pv", 4), sem("b_o_left", 1)
        b_rc, b_nm = sem("b_recip"), sem("b_normalised")
        b_os = [sem(f"b_o_stored{r}", 16) for r in range(2)]

        def b_loads(e, g, p):
            q = [
                e.dma_start(raw(kp[p][1]), k_d[bass.ds(g * HD, HD), :]),
                e.dma_start(raw(qp[p][1]).rearrange("p (h s) -> p h s", h=G),
                            q_d[bass.ds(g * (G * HD), G * HD), :].rearrange("(h p) s -> p h s", p=HD)),
                e.dma_start(raw(vp[p][1])[:, 0:ST, 0:HD], v_d[bass.ds(g * T, S), :].rearrange("(j p) d -> p j d", p=P)),
                e.dma_start(raw(vp[p][1])[0:C, ST, 0:HD], v_d[bass.ds(g * T + S, C), :]),
            ]
            for d in q:
                inc(d, b_ld[p], 16)

        def b_sp_eng(e):
            a_stored(e)
            b_loads(e, 0, 0)

            def body(i, last):
                for hh in range(2 * G):
                    n = i * (2 * G) + hh
                    p, a, r = hh // G, hh % G, hh % 2
                    if a == 0 and not (last and p == 1):
                        g = i * 2 + p
                        hold(e, b_pv, g * G)
                        b_loads(e, g + 1, 1 - p)
                    hold(e, b_oe, n + 1)
                    inc(e.dma_start(o_d[bass.ds(n * HD, HD), :], os_[r]), b_os[r], 16)
                    if last and hh == G - 1:
                        c_first_loads(e)

            with e.Fori(0, NG // 2 - 1) as i:
                body(i, False)
            body(NG // 2 - 1, True)

        def b_pool(e):
            cnt = [0]

            def split(hi, lo, base, done=True):
                inc(e.tensor_copy(hi, raw(lo)), b_ph)
                cnt[0] += 1
                ge(e, b_ph, base + cnt[0])
                m = e.tensor_tensor(lo, raw(lo), raw(hi), ALU.subtract)
                if done:
                    inc(m, b_sp)

            def pieces(names, p, base):
                for nm in names:
                    if nm == "k":
                        split(kp[p][0], kp[p][1], base)
                    elif nm == "v":
                        split(vp[p][0][:, 0:ST, 0:HD], vp[p][1][:, 0:ST, 0:HD], base, False)
                        split(vp[p][0][0:C, ST, 0:HD], vp[p][1][0:C, ST, 0:HD], base)
                    else:
                        a = int(nm[1])
                        split(qp[p][0][:, a * S:(a + 1) * S], qp[p][1][:, a * S:(a + 1) * S], base)

            hold(e, b_ld[0], 64)
            pieces(["k", "q0", "v", "q1", "q2", "q3"], 0, 0)
            per = cnt[0]

            def body(i, last):
                for hh in range(2 * G):
                    n = i * (2 * G) + hh
                    p, a, r = hh // G, hh % G, hh % 2
                    if not (last and p == 1):
                        if a == 0:
                            cnt[0] = 0
                            hold(e, b_ld[1 - p], (i + 1 + p) * 64)
                        pieces([["k", "q0"], ["v", "q1"], ["q2"], ["q3"]][a], 1 - p, (i * 2 + p + 1) * per)

            with e.Fori(0, NG // 2 - 1) as i:
                body(i, False)
            body(NG // 2 - 1, True)

        b_ph = sem("b_pool_hi")

        def b_pe(e):
            def scores(m, p, a, u):
                if u == 0:
                    ge(e, b_sp, six(m, a) + [2, 4, 5, 6][a])
                ge(e, b_ex, m * ST + u - 1)
                qh, ql = (t[:, a * S + u * P:a * S + (u + 1) * P] for t in qp[p])
                parts3(e, su[u % 2][:, 0:S], qh, ql, kp[p][0][:, 0:S], kp[p][1][:, 0:S], True, True)
                inc(parts3(e, su[u % 2][:, S:T], qh, ql, kp[p][0][:, S:T], kp[p][1][:, S:T], True, True), b_S)

            def transp(n, hp, j):
                if j == 0:
                    ge(e, b_nm, n * ST + ST)
                if j != 2:
                    wait = hold if j == ST else ge
                    wait(e, b_lo, n * NT + [-1, 0, 0, 1, 2][j])
                w = P if j < ST else C
                for u in range(ST):
                    m = e.transpose(PS[0:w, TB[j], u * P:(u + 1) * P], pu[hp][u][:, j * P:j * P + w], ident[:])
                inc(m, b_T)

            def pv(n, p, a, j):
                if j == 0:
                    ge(e, b_oe, n)
                    if a == 0:
                        ge(e, b_sp, six(n, a) + 3)
                ge(e, b_lo, n * NT + j + 1)
                w = P if j < ST else C
                vh, vl = (t[0:w, j, :] for t in vp[p])
                ph, pl = (t[0:w, :] for t in pt[j])
                m = parts3(e, PS[0:HD, 7, :], vh, vl, ph, pl, j == 0, j == NT - 1)
                if j == NT - 1:
                    inc(m, b_pv)

            cur = [0, 0]

            def six(m, a):
                return cur[1]

            def body(i, last):
                for hh in range(2 * G):
                    n = i * (2 * G) + hh
                    p, a = hh // G, hh % G
                    nx = None if (last and hh == 2 * G - 1) else n + 1
                    pn, an = ((hh + 1) // G) % 2, (hh + 1) % G
                    gn = i * 2 + (hh + 1) // G

                    def s(u):
                        if nx is not None:
                            cur[1] = gn * 6
                            scores(nx, pn, an, u)

                    def v(j):
                        cur[1] = (i * 2 + p) * 6
                        pv(n, p, a, j)

                    hp = hh % 2
                    for step in ("t0", "s0", "t1", "s1", "t2", "v0", "s2", "t3", "v1", "s3", "t4", "v2", "v3", "v4"):
                        q = int(step[1])
                        {"t": lambda: transp(n, hp, q), "s": lambda: s(q), "v": lambda: v(q)}[step[0]]()

            ge(e, wb_lo, QC)
            cur[1] = 0
            for u in range(ST):
                scores(0, 0, 0, u)
            with e.Fori(0, NG // 2 - 1) as i:
                body(i, False)
            body(NG // 2 - 1, True)

        def b_act(e):
            def exps(m, mp, u):
                if u == 0:
                    ge(e, b_T, (m - 1) * NT)
                ge(e, b_mx, m * ST + u + 1)
                inc(e.activation(pu[mp][u], su[u % 2][:, 0:T], ACT.Exp, bias=negmax[:, mp * ST + u:mp * ST + u + 1],
                                 accum_out=rsum[:, mp * ST + u:mp * ST + u + 1]), b_ex)

            def hi(n, j):
                ge(e, b_T, n * NT + j + 1)
                if j == 0:
                    ge(e, b_pv, n)
                w = P if j < ST else C
                inc(e.activation(pt[j][0][0:w, :], PS[0:w, TB[j], :], ACT.Copy), b_hi)

            def body(i, last):
                for hh in range(2 * G):
                    n = i * (2 * G) + hh
                    r = hh % 2
                    nx = not (last and hh == 2 * G - 1)
                    for j in range(NT):
                        hi(n, j)
                        if j < ST and nx:
                            exps(n + 1, (hh + 1) % 2, j)
                    ge(e, b_pv, n + 1)
                    ge(e, b_os[r], i * (16 * G) + 16 * (hh // 2))
                    inc(e.activation(os_[r], PS[0:HD, 7, :], ACT.Copy), b_oe)

            for u in range(ST):
                exps(0, 0, u)
            with e.Fori(0, NG // 2 - 1) as i:
                body(i, False)
            body(NG // 2 - 1, True)

        def b_dve(e):
            def mx(m, mp, u):
                ge(e, b_S, m * ST + u + 1)
                inc(e.tensor_reduce(negmax[:, mp * ST + u:mp * ST + u + 1], su[u % 2][:, 0:T], AX.X, ALU.max, negate=True), b_mx)

            def norm(m, mp, u):
                c = slice(mp * ST + u, mp * ST + u + 1)
                ge(e, b_ex, m * ST + u + 1)
                inc(e.reciprocal(rrec[:, c], rsum[:, c]), b_rc)
                ge(e, b_rc, m * ST + u + 1)
                inc(e.tensor_scalar(pu[mp][u], pu[mp][u], rrec[:, c], None, ALU.mult), b_nm)

            def lo(n, j):
                ge(e, b_hi, n * NT + j + 1)
                w = P if j < ST else C
                inc(e.tensor_tensor(pt[j][1][0:w, :], PS[0:w, TB[j], :], raw(pt[j][0][0:w, :]), ALU.subtract), b_lo)

            def body(i, last):
                for hh in range(2 * G):
                    n = i * (2 * G) + hh
                    nx = not (last and hh == 2 * G - 1)
                    mp = (hh + 1) % 2
                    for j in range(NT):
                        lo(n, j)
                        if nx:
                            if j < ST:
                                mx(n + 1, mp, j)
                            if j >= 1:
                                norm(n + 1, mp, j - 1)

            for u in range(ST):
                mx(0, 0, u)
                norm(0, 0, u)
            with e.Fori(0, NG // 2 - 1) as i:
                body(i, False)
            body(NG // 2 - 1, True)

        halves = [SF[:, h * NB:(h + 1) * NB] for h in range(2)]
        j_ld = [sem(f"job_raw{h}") for h in range(2)]
        j_hi, j_lo = sem("job_hi"), sem("job_lo", 2)
        up_v = up_w.rearrange("(k p) n -> p k n", p=P)
        fc_v = fc1_w.rearrange("(k p) n -> p k n", p=P)

        def job_src(j, h):
            kind, c = j
            if kind == "e":
                w, c = (down_w, c) if c < FC else (w_d, c - FC)
                return w[c * P:(c + 1) * P, h * NB:(h + 1) * NB]
            return (up_v if kind == "u" else fc_v)[:, h * (DK // 2):(h + 1) * (DK // 2), c * P:(c + 1) * P]

        def job_slot(j):
            return FC + j[1] % 2 if j[0] == "f" else j[1]

        def job_load(e, j, m):
            for h in range(2):
                src = job_src(j, h)
                hold(e, j_lo, m * 2 + h - 1)
                o = halves[h] if len(src.shape) == 2 else halves[h].rearrange("p (k e) -> p k e", k=DK // 2)
                inc(e.dma_start(o, src), j_ld[h], 16)

        def job_part(j, h, part):
            return part(job_slot(j))[:, h * NB:(h + 1) * NB]

        def job_hi(e, j, m, free=None):
            if free:
                free()
            for h in range(2):
                ge(e, j_ld[h], m * 16 + 16)
                inc(e.activation(job_part(j, h, slot_hi), halves[h], ACT.Copy), j_hi)

        def job_lo(e, j, m, done):
            for h in range(2):
                ge(e, j_hi, m * 2 + h + 1)
                inc(e.tensor_tensor(job_part(j, h, slot_lo), halves[h], raw(job_part(j, h, slot_hi)), ALU.subtract), j_lo)
            ge(e, j_lo, m * 2 + 2)
            e.sem_inc(sems[done][0], 1)

        D_GROUPS = [[("u", 0), ("u", 1), ("u", 2)], [("u", 3), ("u", 4), ("u", 5)], [("f", 0), ("u", 6), ("u", 7)],
                    [("f", 1), ("u", 8), ("u", 9)], [("f", 2), ("u", 10), ("u", 11)], [("u", 12), ("u", 13)],
                    [("f", 3), ("u", 14), ("u", 15)]]
        JOBS_C = {0: [("u", 0), ("u", 1)], 1: [("u", 2), ("u", 3)], 2: [("u", 4)], 3: [("u", 5)]}
        JOBS_FIRST = {-1: D_GROUPS[2], 0: D_GROUPS[3], 1: [("u", 10), ("u", 11)], 2: [("f", 2), ("u", 12), ("u", 13)],
                      3: D_GROUPS[6], 4: [("f", 0)]}
        JOBS_MID = {-1: [("f", 1)], 2: [("f", 2)], 3: [("f", 3)], 4: [("f", 0)]}
        JOBS_LAST = {-1: [("f", 1)], 0: [("e", 0), ("e", 1), ("e", 2)], 1: [("e", 3), ("e", 4), ("e", 5)],
                     2: [("f", 2), ("e", 6), ("e", 7)], 3: [("f", 3), ("e", 8), ("e", 9)], 4: [("e", 10), ("e", 11)],
                     5: [("e", 12), ("e", 13)], 6: [("e", 14), ("e", 15)]}

        def flat(jobs):
            return [(at, j) for at in sorted(jobs) for j in jobs[at]]

        N_C = len(flat(JOBS_C))
        N_FIRST = len(flat(JOBS_FIRST))
        N_MID = len(flat(JOBS_MID))
        N_LAST = len(flat(JOBS_LAST))
        M_FIRST = N_C
        M_MID = M_FIRST + N_FIRST
        M_LAST = M_MID + N_MID * (B - 2)
        M_E = M_LAST + N_LAST
        d_up, d_fc, e_sl = sem("d_up_slots"), sem("d_fc_slots"), sem("e_slots")
        DONE = {"u": d_up, "f": d_fc, "e": e_sl}

        CU = QC // 4
        cu = [[mmf(QB + (2 * u + i) * CU * P, CU * P).rearrange("p (c s) -> p c s", c=CU) for i in range(2)] for u in range(4)]
        assert 8 * CU * P <= 2 * G * S
        XR = SF[:, 5 * D:6 * D]
        XN2 = SF[:, D:D + ST * D].rearrange("p (t d) -> p t d", t=ST)
        cc_ld = [sem(f"c_o_loaded{u}") for u in range(4)]
        cc_xl = sem("c_x_loaded")
        cc_hi, cc_lo = sem("c_o_hi"), sem("c_o_lo")
        cc_use, cc_x1 = sem("c_unit_used", 4), sem("c_x1", 2)
        cc_st = sem("c_stored")
        d_acc = sem("d_product", 20)

        d_load, d_norm, d_sqrt, d_pet0, d_hi, d_lo, d_zl, d_fr, d_zt = norm_z(
            "d", XN2, lambda e, b: ge(e, d_acc, b * ND))

        def c_load_unit(e, b, t, u):
            n = b * ST + t
            hold(e, cc_use, n * 4 + u - 3)
            src = o_d[bass.ds(b * E + u * CU * P, CU * P), t * P:(t + 1) * P]
            inc(e.dma_start(raw(cu[u][1]), src.rearrange("(c p) s -> p c s", p=P)), cc_ld[u], 16)

        def c_first_loads(e):
            hold(e, b_pv, (NG - 1) * G)
            for r in range(2):
                ge(e, b_os[r], H // 2 * 16)
            for u in range(4):
                c_load_unit(e, 0, 0, u)

        def c_sp_eng(e):
            def load_x(n):
                inc(e.dma_start(XR, x_r[bass.ds(n * P, P), :]), cc_xl, 16)

            def tiles(b, t0, jobs=None):
                m = 0
                for r in range(2):
                    hold(e, b_os[r], b * (H // 2 * 16) + H // 2 * 16)
                for t in range(t0, ST):
                    n = b * ST + t
                    for u in range(4):
                        c_load_unit(e, b, t, u)
                    hold(e, cc_x1, n)
                    inc(e.dma_start(x1_d[bass.ds(n * P - P, P), :], XR), cc_st, 16)
                    hold(e, cc_st, n * 16)
                    load_x(n)
                    for j in (jobs or {}).get(t, []):
                        job_load(e, j, m)
                        m += 1

            hold(e, b_pv, NH)
            for r in range(2):
                ge(e, b_os[r], NH // 2 * 16)
            load_x(0)
            tiles(0, 1)
            with e.Fori(1, B - 1) as b:
                tiles(b, 0)
            d_load(e, x1_d, 0)
            tiles(B - 1, 0, JOBS_C)
            hold(e, cc_x1, B * ST)
            inc(e.dma_start(x1_d[(B * ST - 1) * P:B * ST * P, :], XR), cc_st, 16)
            ge(e, cc_st, B * ST * 16)

        def c_act(e):
            def tiles(b, jobs=None):
                m = 0
                for t in range(ST):
                    n = b * ST + t
                    for u in range(4):
                        ge(e, cc_ld[u], n * 16 + 16)
                        inc(e.activation(cu[u][0], raw(cu[u][1]), ACT.Copy), cc_hi)
                    for j in (jobs or {}).get(t, []):
                        job_hi(e, j, m)
                        m += 1

            with e.Fori(0, B - 1) as b:
                tiles(b)
            d_sqrt(e, 0)
            tiles(B - 1, JOBS_C)

        def c_pool(e):
            def tiles(b, jobs=None):
                m = 0
                for t in range(ST):
                    n = b * ST + t
                    for u in range(4):
                        ge(e, cc_hi, n * 4 + u + 1)
                        inc(e.tensor_tensor(cu[u][1], raw(cu[u][1]), raw(cu[u][0]), ALU.subtract), cc_lo)
                    for j in (jobs or {}).get(t, []):
                        job_lo(e, j, m, DONE[j[0]])
                        m += 1

            with e.Fori(0, B - 1) as b:
                tiles(b)
            tiles(B - 1, JOBS_C)

        def c_pe(e):
            ge(e, b_ex, NH * ST)
            with e.Fori(0, B) as b:
                for t in range(ST):
                    n = b * ST + t
                    ge(e, cc_x1, n - 1)
                    for k in range(QC):
                        u, c = k // CU, k % CU
                        if c == 0:
                            ge(e, cc_lo, n * 4 + u + 1)
                        wh, wl = slot_hi(WO0 + k), slot_lo(WO0 + k)
                        for h in range(2):
                            hs = slice(h * NB, (h + 1) * NB)
                            m = parts3(e, PS[:, 2 * (t % 2) + h, :], cu[u][0][:, c, :], cu[u][1][:, c, :],
                                       wh[:, hs], wl[:, hs], k == 0, k == QC - 1)
                        if c == CU - 1:
                            inc(m, cc_use)

        def c_dve(e):
            def tiles(b):
                for t in range(ST):
                    n, r = b * ST + t, t % 2
                    ge(e, cc_use, n * 4 + 4)
                    ge(e, cc_xl, n * 16 + 16)
                    inc(e.tensor_tensor(XR, PS[:, 2 * r:2 * r + 2, :].rearrange("p b n -> p (b n)"), XR, ALU.add), cc_x1)

            with e.Fori(0, B - 1) as b:
                tiles(b)
            d_norm(e, 0)
            tiles(B - 1)

        st2 = [SF[:, 5 * D + r * NB:5 * D + (r + 1) * NB] for r in range(2)]
        D_ALL = [c for g in D_GROUPS for c in g]
        D_CUM = [sum(len(x) for x in D_GROUPS[:g + 1]) for g in range(len(D_GROUPS))]
        ND = len(D_ALL)
        assert ND == FC + LC == 20 and FC == 16 and LC == 4
        d_ev, d_sq = sem("d_staged", 1), sem("d_squared")
        d_st = [sem(f"d_stored{r}", 16) for r in range(2)]
        d_gm, d_gc = sem("d_gate_product"), sem("d_gate_chain", 1)
        d_gw = sem("d_gate_weights")
        GC = 7

        def jobs_of(b):
            if isinstance(b, int):
                return (JOBS_FIRST, M_FIRST) if b == 0 else (JOBS_LAST, M_LAST)
            return JOBS_MID, b * N_MID + (M_MID - N_MID)

        def d_sp_eng(e):
            for b in (0, None, B - 1):
                def run(b, n_before):
                    for m, (at, j) in enumerate(flat(jobs_of(b)[0])):
                        job_load(e, j, n_before + m)

                if b is not None:
                    run(b, jobs_of(b)[1])
                else:
                    with e.Fori(1, B - 1) as r:
                        run(r, jobs_of(r)[1])

        def d_pool(e):
            for b in (0, None, B - 1):
                def run(b, n_before):
                    for m, (at, j) in enumerate(flat(jobs_of(b)[0])):
                        job_lo(e, j, n_before + m, DONE[j[0]])

                if b is not None:
                    run(b, jobs_of(b)[1])
                else:
                    with e.Fori(1, B - 1) as r:
                        run(r, jobs_of(r)[1])

        def d_pe(e):
            def pet(e, b, k):
                if k == 0:
                    ge(e, d_gc, b * GC)
                d_pet0(e, b, k)

            ge(e, cc_x1, B * ST)
            with e.Fori(0, B) as b:
                def wait_bank(g):
                    ge(e, d_ev, b * ND + (D_CUM[g - 2] if g >= 2 else 0))

                def slot_ready(ch):
                    if ch[0] == "u":
                        ge(e, d_up, ch[1] + 1)
                    else:
                        ge(e, d_fc, b * LC + ch[1] + 1)

                def gate(g):
                    if g:
                        return
                    ge(e, d_gw, 18)
                    for t in range(ST):
                        ts = slice(t * P, (t + 1) * P)
                        for k in range(DK):
                            e.matmul(PS[:, 6, t * 2 * NE:(t + 1) * 2 * NE], zhi[:, k, ts], GW[:, k, :], start=k == 0, stop=False)
                            m = e.matmul(PS[:, 6, t * 2 * NE:t * 2 * NE + NE], zlo[:, k, ts], GW[:, k, 0:NE],
                                         start=False, stop=k == DK - 1)
                    inc(m, d_gm)

                mm_groups(e, b, D_GROUPS, d_zl, pet, wait_bank, job_slot, d_acc, slot_ready, gate, d_fr)

        def d_act(e):
            def body(b, last):
                jobs, m0 = jobs_of(b)
                m = [0]

                def run(at, b):
                    for j in jobs.get(at, []):
                        done_before = {("f", 0): (0, 4), ("f", 1): (-1, 6), ("f", 2): (0, 2), ("f", 3): (0, 3)}
                        free = None
                        if j[0] == "e":
                            free = lambda: ge(e, d_acc, b * ND + D_ALL.index(("u", j[1])) + 1)
                        elif j[0] == "f" and not (isinstance(b, int) and b == 0 and at <= 0):
                            db, g = done_before[j]
                            free = lambda: ge(e, d_acc, (b + db) * ND + D_CUM[g])
                        elif at == -1:
                            free = lambda: ge(e, cc_use, B * ST * 4)
                        job_hi(e, j, m0 + m[0], free)
                        m[0] += 1

                for k in range(DK):
                    d_hi(e, b, k)
                run(-1, b)
                n, sq = 0, 0
                for g, chunks in enumerate(D_GROUPS):
                    for c, ch in enumerate(chunks):
                        r = n % 2
                        ge(e, d_acc, b * ND + n + 1)
                        ge(e, d_st[r], b * (16 * ND // 2) + 16 * (n // 2))
                        up = ch[0] == "u"
                        inc(e.activation(st2[r], PS[:, 3 * (g % 2) + c, :], ACT.Relu if up else ACT.Copy), d_ev)
                        if up:
                            sq += 1
                            ge(e, d_sq, b * FC + sq)
                        else:
                            ge(e, d_ev, b * ND + n + 1)
                        row = ch[1] * P if up else F + ch[1] * P
                        inc(e.dma_start(h_d[bass.ds(b * (F + L) + row, P), :], st2[r]), d_st[r], 16)
                        n += 1
                    run(g, b)
                    if g == 0 and not last:
                        d_load(e, x1_d, b + 1)
                    if g == 2 and not last:
                        d_sqrt(e, b + 1)

            body(0, False)
            with e.Fori(1, B - 1) as b:
                body(b, False)
            body(B - 1, True)
            for r in range(2):
                ge(e, d_st[r], B * (16 * ND // 2))

        def d_dve(e):
            def body(b, last):
                for k in range(DK):
                    d_lo(e, b, k)
                n = 0
                for g, chunks in enumerate(D_GROUPS):
                    for ch in chunks:
                        if ch[0] == "u":
                            r = n % 2
                            ge(e, d_ev, b * ND + n + 1)
                            inc(e.tensor_tensor(st2[r], st2[r], st2[r], ALU.mult), d_sq)
                        n += 1
                    if g == 0:
                        hold(e, d_gm, b + 1)
                        q = [0]

                        def link(ins):
                            q[0] += 1
                            inc(ins, d_gc)
                            hold(e, d_gc, b * GC + q[0])

                        link(e.tensor_copy(gsum.rearrange("p t e -> p (t e)"), PS[:, 6, 0:ST * 2 * NE]))
                        link(e.tensor_tensor(g8, gsum[:, :, 0:NE], gsum[:, :, NE:2 * NE], ALU.add))
                        for t in range(ST):
                            link(e.max(gtop[:, t, :], g8[:, t, :]))
                        link(e.tensor_tensor(rw[:, bass.ds(b * ST, ST)], gtop[:, :, 0], gtop[:, :, 1], ALU.add))
                        assert q[0] == GC
                    if g == 2 and not last:
                        d_norm(e, b + 1)

            ge(e, d_gw, 16)
            inc(e.tensor_copy(GW[:, :, 0:NE], graw), d_gw)
            ge(e, d_gw, 17)
            inc(e.tensor_tensor(GW[:, :, NE:2 * NE], graw, raw(GW[:, :, 0:NE]), ALU.subtract), d_gw)
            with e.Fori(0, B - 1) as b:
                body(b, False)
            body(B - 1, True)

        NK = FC + LC
        EU = NK // 4
        H0 = NK * SLOT
        eu = [[mmf(H0 + (2 * u + i) * EU * P, EU * P).rearrange("p (c s) -> p c s", c=EU) for i in range(2)] for u in range(4)]
        x1b = SF[:, D:2 * D]
        yb = [SF[:, (2 + r) * D:(3 + r) * D] for r in range(2)]
        gam, bet = SF[:, 4 * D:5 * D], SF[:, 5 * D:6 * D]
        e_ld = [sem(f"e_h_loaded{u}") for u in range(4)]
        e_hi, e_lo, e_use = sem("e_h_hi"), sem("e_h_lo"), sem("e_unit_used", 4)
        e_y, e_add, e_sq, e_ch = sem("e_routed"), sem("e_added", 2), sem("e_sqrt"), sem("e_chain")
        e_post = sem("e_post", 1)
        e_gb, e_xl = sem("e_gamma_beta"), sem("e_x1_loaded")
        e_st = [sem(f"e_stored{r}", 16) for r in range(2)]
        E_CHAIN = 13

        def e_load(e, b, t, u):
            n = b * ST + t
            hold(e, e_use, n * 4 + u - 3)
            src = h_d[bass.ds(b * (F + L) + u * EU * P, EU * P), t * P:(t + 1) * P]
            inc(e.dma_start(raw(eu[u][1]), src.rearrange("(c p) s -> p c s", p=P)), e_ld[u], 16)

        def e_load_x1(e, n):
            hold(e, e_post, n)
            inc(e.dma_start(x1b, x1_d[bass.ds(n * P, P), :]), e_xl, 16)

        def e_sp_eng(e):
            for r in range(2):
                ge(e, d_st[r], B * (16 * ND // 2))
            hold(e, d_acc, B * ND)
            for u in range(4):
                e_load(e, 0, 0, u)
            for m in range(LC):
                job_load(e, ("e", FC + m), M_E + m)
            inc(e.dma_start(gam, gamma.partition_broadcast(P)), e_gb, 16)
            inc(e.dma_start(bet, beta.partition_broadcast(P)), e_gb, 16)
            e_load_x1(e, 0)

            def rest(b, t0):
                for t in range(t0, ST):
                    for u in range(4):
                        e_load(e, b, t, u)
                    e_load_x1(e, b * ST + t)

            rest(0, 1)
            with e.Fori(1, B) as b:
                rest(b, 0)

        def e_pool(e):
            def split(n, u):
                ge(e, e_hi, n * 4 + u + 1)
                inc(e.tensor_tensor(eu[u][1], raw(eu[u][1]), raw(eu[u][0]), ALU.subtract), e_lo)

            for u in range(4):
                split(0, u)
            for m in range(LC):
                job_lo(e, ("e", FC + m), M_E + m, e_sl)
            for t in range(1, ST):
                for u in range(4):
                    split(t, u)
            with e.Fori(1, B) as b:
                for t in range(ST):
                    for u in range(4):
                        split(b * ST + t, u)

        def e_pe(e):
            ge(e, d_ev, B * ND)
            ge(e, d_gc, B * GC)
            with e.Fori(0, B) as b:
                for t in range(ST):
                    n = b * ST + t
                    ge(e, e_add, n - 1)
                    for k in range(NK):
                        u, c = k // EU, k % EU
                        if c == 0:
                            ge(e, e_lo, n * 4 + u + 1)
                        if t == 0:
                            ge(e, e_sl, k + 1)
                        wh, wl = slot_hi(k), slot_lo(k)
                        for h in range(2):
                            hs = slice(h * NB, (h + 1) * NB)
                            bank = 4 * (t % 2) + (0 if k < FC else 2) + h
                            m = parts3(e, PS[:, bank, :], eu[u][0][:, c, :], eu[u][1][:, c, :],
                                       wh[:, hs], wl[:, hs], k in (0, FC), k in (FC - 1, NK - 1))
                        if c == EU - 1:
                            inc(m, e_use)

        def bank2(i):
            return PS[:, i:i + 2, :].rearrange("p b n -> p (b n)")

        def e_act(e):
            def hi(n, u):
                ge(e, e_ld[u], n * 16 + 16)
                inc(e.activation(eu[u][0], raw(eu[u][1]), ACT.Copy), e_hi)

            def step(b, t, more):
                n, r = b * ST + t, t % 2
                if more:
                    for u in range(3):
                        hi(n + 1, u)
                ge(e, e_use, n * 4 + 4)
                ge(e, e_st[r], b * (16 * ST // 2) + 16 * (t // 2))
                inc(e.activation(yb[r], bank2(4 * r + 2), ACT.Copy, scale=rw[:, bass.ds(n, 1)]), e_y)
                if more:
                    hi(n + 1, 3)
                ge(e, e_ch, n * E_CHAIN + 6)
                inc(e.activation(rt[:, 0:1], rec[:, 0:1], ACT.Sqrt), e_sq)
                ge(e, e_post, n + 1)
                inc(e.dma_start(out_r[bass.ds(n * P, P), :], yb[r]), e_st[r], 16)

            for u in range(4):
                hi(0, u)
            for m in range(LC):
                job_hi(e, ("e", FC + m), M_E + m)
            with e.Fori(0, B - 1) as b:
                for t in range(ST):
                    step(b, t, True)
            for t in range(ST):
                step(B - 1, t, t < ST - 1)
            for r in range(2):
                ge(e, e_st[r], B * (16 * ST // 2))

        def e_dve(e):
            ge(e, e_gb, 32)
            with e.Fori(0, B) as b:
                for t in range(ST):
                    n, r = b * ST + t, t % 2
                    q = [0]

                    def link(ins, last=True):
                        q[0] += 1
                        inc(ins, e_ch)
                        if last:
                            hold(e, e_ch, n * E_CHAIN + q[0])

                    ge(e, e_y, n + 1)
                    inc(e.tensor_tensor(yb[r], bank2(4 * r), yb[r], ALU.add), e_add)
                    ge(e, e_add, n + 1)
                    for h in range(2):
                        link(e.bn_stats(stats[:, 0, h, :], yb[r][:, h * NB:(h + 1) * NB]), h == 1)
                    link(e.bn_aggr(mv[:, 0, :], stats[:, 0, :, :]))
                    link(e.tensor_scalar(ve[:, 0:1], mv[:, 0, 1:2], EPS, None, ALU.add))
                    link(e.reciprocal(rec[:, 0:1], ve[:, 0:1]))
                    link(e.tensor_scalar(rec[:, 1:2], ve[:, 0:1], -0.5, None, ALU.mult))
                    hold(e, e_sq, n + 1)
                    link(e.tensor_tensor(nt1[:, 0:1], rt[:, 0:1], rt[:, 0:1], ALU.mult))
                    link(e.tensor_tensor(nt1[:, 0:1], nt1[:, 0:1], rec[:, 1:2], ALU.mult))
                    link(e.tensor_scalar(nt1[:, 0:1], nt1[:, 0:1], 1.5, None, ALU.add))
                    link(e.tensor_tensor(rstd[:, 0:1], rt[:, 0:1], nt1[:, 0:1], ALU.mult))
                    link(e.tensor_scalar(yb[r], yb[r], mv[:, 0, 0:1], rstd[:, 0:1], ALU.subtract, ALU.mult))
                    link(e.tensor_tensor(yb[r], yb[r], gam, ALU.mult))
                    link(e.tensor_tensor(yb[r], yb[r], bet, ALU.add))
                    assert q[0] == E_CHAIN
                    ge(e, e_xl, n * 16 + 16)
                    inc(e.tensor_tensor(yb[r], yb[r], x1b, ALU.add), e_post)

        block = es.enter_context(nc.Block())

        @block.sync
        def _(e):
            fold_sp(e)
            fold_store(e)
            ctx_sp(e)
            wa_sp(e)
            a_sp(e)
            hold(e, a_zt, B * DK)
            inc(e.dma_start(graw, gate_w.rearrange("(k p) e -> p k e", p=P)), d_gw, 16)
            wb_sp(e)
            b_sp_eng(e)
            c_sp_eng(e)
            d_sp_eng(e)
            e_sp_eng(e)

        @block.gpsimd
        def _(e):
            for h, credit in sems.values():
                if credit:
                    e.sem_inc(h, credit)
            inc(e.memset(ident[:], 0.0), ph_start)
            ge(e, ph_start, 1)
            inc(e.affine_select(out=ident[:], in_=ident[:], compare_op=ALU.not_equal, fill=1.0, base=0,
                                pattern=[[-1, P]], channel_multiplier=1), ph_start)
            b_pool(e)
            c_pool(e)
            d_pool(e)
            e_pool(e)

        @block.scalar
        def _(e):
            fold_act(e)
            fold_evac(e)
            wa_act(e)
            ctx_act(e)
            a_act(e)
            wb_act(e)
            b_act(e)
            c_act(e)
            d_act(e)
            e_act(e)

        @block.vector
        def _(e):
            fold_dve(e)
            wa_dve(e)
            ctx_dve(e)
            a_dve(e)
            wb_dve(e)
            b_dve(e)
            c_dve(e)
            d_dve(e)
            e_dve(e)

        @block.tensor
        def _(e):
            fold_pe(e)
            ge(e, f_ev, 1)
            wa_pe(e)
            ctx_pe(e)
            a_pe(e)
            ge(e, a_ev, B * A_EV)
            wb_pe(e)
            b_pe(e)
            c_pe(e)
            d_pe(e)
            e_pe(e)


_P = "L0_xattn_"
_F = "L0_ffn_"


def kernel(**inputs):
    import numpy as np
    import concourse.bacc as bacc
    from concourse.bass_utils import run_bass_kernel_spmd

    arrays = {
        "x": inputs["x"],
        "ctx": inputs["ctx_4096"],
        "wqkv": np.concatenate([np.asarray(inputs[_P + w]) for w in ("Wq", "Wk", "Wv")], axis=0),
        "wo": inputs[_P + "Wo"],
        "gate_w": inputs[_F + "gate_w"],
        "up_w": inputs[_F + "up_w"],
        "down_w": inputs[_F + "down_w"],
        "fc1_w": inputs[_F + "fc1_w"],
        "fc2_w": inputs[_F + "fc2_w"],
        "expert_w": inputs[_F + "expert_w"],
        "gamma": inputs[_F + "ln_gamma"],
        "beta": inputs[_F + "ln_beta"],
    }
    arrays = {f"in_{k}": np.ascontiguousarray(v) for k, v in arrays.items()}
    nc = bacc.Bacc("TRN2", target_bir_lowering=False, num_devices=1)
    aps = [nc.dram_tensor(k, v.shape, mybir.dt.from_np(v.dtype), kind="ExternalInput").ap() for k, v in arrays.items()]
    out = nc.dram_tensor("out", arrays["in_x"].shape, mybir.dt.float32, kind="ExternalOutput").ap()
    xattn_ffn_kernel(nc, *aps, out)
    r = run_bass_kernel_spmd(nc, [arrays], core_ids=[0])
    return r.results[0]["out"]
```

```python
import concourse.bass as bass
from concourse import mybir
from contextlib import ExitStack


def xattn_ffn_kernel(nc, x, ctx, wqkv, wo, gate_w, up_w, down_w, fc1_w, fc2_w, expert_w, gamma, beta, out):
    f32 = mybir.dt.float32
    f32r = mybir.dt.float32r
    ALU = mybir.AluOpType
    ACT = mybir.ActivationFunctionType
    AX = mybir.AxisListType

    P = 128
    B, S, D = x.shape
    C = ctx.shape[1]
    T = S + C
    HD = 96
    E = wo.shape[1]
    H = E // HD
    KVE = (wqkv.shape[0] - E) // 2
    KV = KVE // HD
    G = H // KV
    F = up_w.shape[1]
    L = fc1_w.shape[1]
    NE = gate_w.shape[1]
    EPS = 1e-5
    SCALE = float(HD) ** -0.5

    DK = D // P
    ST = S // P
    NT = T // P + 1
    QC, KC = E // P, KVE // P
    FC, LC = F // P, L // P
    NB = S
    assert D == 1024 and S == 512 and C == 64 and NT == 5 and KC == 3 and QC == 12 and G == 4

    def dram(name, shape):
        return nc.dram_tensor(name, shape, f32, kind="Internal").ap()

    q_d = dram("q_scratch", (B * E, S))
    k_d = dram("k_scratch", (B * KVE, T))
    v_d = dram("v_scratch", (B * KV * T, HD))
    o_d = dram("o_scratch", (B * E, S))
    x1_d = dram("x1_scratch", (B * S, D))
    h_d = dram("h_scratch", (B * (F + L), S))
    w_d = dram("fold_scratch", (L, D))

    x_r = x.rearrange("b s d -> (b s) d")
    out_r = out.rearrange("b s d -> (b s) d")

    es = ExitStack()
    with es:
        SLOT = 2 * D
        MM = es.enter_context(nc.sbuf_tensor("operands", [P, 22 * SLOT + 1024], f32r))
        SF = es.enter_context(nc.sbuf_tensor("staging", [P, 6656], f32))
        ident = es.enter_context(nc.sbuf_tensor("ident", [P, P], f32))
        sm = es.enter_context(nc.sbuf_tensor("small", [P, 344], f32))
        PS = es.enter_context(nc.psum_tensor("psum", [P, 8, NB], f32))

        def mmf(a, n, p=P, p0=0):
            return MM[p0:p0 + p, a:a + n]

        def raw(ap):
            return ap.bitcast(f32)

        def slot_hi(s):
            return mmf(s * SLOT, D)

        def slot_lo(s):
            return mmf(s * SLOT + D, D)

        Z0 = 18 * SLOT
        zhi = mmf(Z0, DK * S).rearrange("p (k s) -> p k s", k=DK)
        zlo = mmf(Z0 + DK * S, DK * S).rearrange("p (k s) -> p k s", k=DK)

        GW = mmf(22 * SLOT, DK * 2 * NE).rearrange("p (k e) -> p k e", k=DK)

        stats = sm[:, 0:48].rearrange("p (t h s) -> p t h s", t=4, h=2)
        mv = sm[:, 48:56].rearrange("p (t s) -> p t s", t=4)
        ve, rec, rt, nt1, rstd = (sm[:, 56 + 4 * i:60 + 4 * i] for i in range(5))
        negmax = sm[:, 80:88]
        gsum = sm[:, 88:152].rearrange("p (t e) -> p t e", t=4)
        g8 = sm[:, 152:184].rearrange("p (t e) -> p t e", t=4)
        gtop = sm[:, 88:120].rearrange("p (t e) -> p t e", t=4)
        rw = sm[:, 184:200]
        rsum, rrec = sm[:, 296:304], sm[:, 304:312]
        graw = sm[:, 232:296].rearrange("p (k e) -> p k e", k=DK)

        sems = {}

        def sem(name, credit=0):
            s = es.enter_context(nc.semaphore(name))
            sems[name] = (s, credit)
            return name

        def ge(e, name, v):
            s, c = sems[name]
            e.wait_ge(s, v + c)

        def hold(e, name, v):
            ge(e, name, v)
            e.sem_inc(idle, 1)

        def inc(ins, name, n=1):
            ins.then_inc(sems[name][0], n)

        idle = es.enter_context(nc.semaphore("idle"))

        def parts3(e, o, lh, ll, rh, rl, first, last):
            e.matmul(o, lh, rh, start=first, stop=False)
            e.matmul(o, lh, rl, start=False, stop=False)
            return e.matmul(o, ll, rh, start=False, stop=last)

        ph_start = sem("constants_ready")

        def weight_prep(tag, n, src, slot0, raw_at, nb=3):
            ld = [sem(f"{tag}_raw{p}") for p in range(nb)]
            tr = sem(f"{tag}_transposed", nb)
            hi = sem(f"{tag}_hi")
            lo = sem(f"{tag}_lo", nb)
            rawb = [SF[:, raw_at + p * D:raw_at + (p + 1) * D] for p in range(nb)]
            bank = [PS[:, 2 * p:2 * p + 2, :].rearrange("p b n -> p (b n)") for p in range(nb)]
            assert n % nb == 0

            def dst(i, p, off):
                return MM[:, bass.ds(i * (nb * SLOT) + ((slot0 + p) * SLOT + off), D)]

            def sp(e):
                with e.Fori(0, n // nb) as i:
                    for p in range(nb):
                        hold(e, tr, i * nb + p + 1 - nb)
                        view = src(i * nb + p)
                        o = rawb[p] if len(view.shape) == 2 else rawb[p].rearrange("p (i e) -> p i e", e=P)
                        inc(e.dma_start(o, view), ld[p], 16)

            def pe(e):
                with e.Fori(0, n // nb) as i:
                    for p in range(nb):
                        ge(e, ld[p], i * 16 + 16)
                        ge(e, lo, i * nb + p + 1 - nb)
                        for k in range(DK):
                            m = e.transpose(bank[p][:, k * P:(k + 1) * P], rawb[p][:, k * P:(k + 1) * P], ident[:])
                        inc(m, tr)

            def act(e):
                with e.Fori(0, n // nb) as i:
                    for p in range(nb):
                        ge(e, tr, i * nb + p + 1)
                        inc(e.activation(dst(i, p, 0), bank[p], ACT.Copy), hi)

            def dve(e):
                with e.Fori(0, n // nb) as i:
                    for p in range(nb):
                        ge(e, hi, i * nb + p + 1)
                        inc(e.tensor_tensor(dst(i, p, D), bank[p], raw(dst(i, p, 0)), ALU.subtract), lo)

            return sp, pe, act, dve, lo, tr

        LN_CHAIN = 18

        def norm_z(tag, xn, last_free):
            ld = sem(f"{tag}_x")
            ch = sem(f"{tag}_chain")
            sq = sem(f"{tag}_sqrt")
            zn = sem(f"{tag}_z")
            zt = sem(f"{tag}_zt", 8)
            zh = sem(f"{tag}_zhi")
            zl = sem(f"{tag}_zlo", 8)
            fr = sem(f"{tag}_zfree", DK)

            def load(e, src, b):
                hold(e, zt, b * DK)
                inc(e.dma_start(xn, src[bass.ds(b * S, S), :].rearrange("(t p) d -> p t d", p=P)), ld, 16)

            def dve_norm(e, b):
                n = [0]

                def link(ins, last=True):
                    n[0] += 1
                    inc(ins, ch)
                    if last:
                        hold(e, ch, b * LN_CHAIN + n[0])

                hold(e, ld, b * 16 + 16)
                for t in range(ST):
                    for h in range(2):
                        link(e.bn_stats(stats[:, t, h, :], xn[:, t, h * NB:(h + 1) * NB]), (t, h) == (ST - 1, 1))
                for t in range(ST):
                    link(e.bn_aggr(mv[:, t, :], stats[:, t, :, :]), t == ST - 1)
                link(e.tensor_scalar(ve, mv[:, :, 1], EPS, None, ALU.add))
                link(e.reciprocal(rec, ve))
                hold(e, sq, b + 1)
                link(e.tensor_tensor(nt1, rt, rt, ALU.mult))
                link(e.tensor_tensor(nt1, nt1, ve, ALU.mult))
                link(e.tensor_scalar(nt1, nt1, -0.5, 1.5, ALU.mult, ALU.add))
                link(e.tensor_tensor(rstd, rt, nt1, ALU.mult))
                assert n[0] == LN_CHAIN
                for t in range(ST):
                    z = e.tensor_scalar(xn[:, t, :], xn[:, t, :], mv[:, t, 0:1], rstd[:, t:t + 1], ALU.subtract, ALU.mult)
                inc(z, zn)

            def act_sqrt(e, b):
                ge(e, ch, b * LN_CHAIN + 14)
                inc(e.activation(rt, rec, ACT.Sqrt), sq)

            def pe_t(e, b, k):
                if k == 0:
                    ge(e, zn, b + 1)
                ge(e, zl, b * DK + k - 1)
                for t in range(ST):
                    m = e.transpose(PS[:, 6 + k % 2, t * P:(t + 1) * P], xn[:, t, k * P:(k + 1) * P], ident[:])
                inc(m, zt)

            def act_hi(e, b, k):
                ge(e, zt, b * DK + k + 1)
                if k < DK - 1:
                    ge(e, fr, (b - 1) * (DK - 1) + k + 1)
                else:
                    last_free(e, b)
                inc(e.activation(zhi[:, k, :], PS[:, 6 + k % 2, :], ACT.Copy), zh)

            def dve_lo(e, b, k):
                ge(e, zh, b * DK + k + 1)
                inc(e.tensor_tensor(zlo[:, k, :], PS[:, 6 + k % 2, :], raw(zhi[:, k, :]), ALU.subtract), zl)

            return load, dve_norm, act_sqrt, pe_t, act_hi, dve_lo, zl, fr, zt

        def mm_groups(e, b, groups, lo_sem, wait_bank, slot_of, done, slot_ready=None, after_group=None, free=None, pe_t=None):
            for g, chunks in enumerate(groups):
                last = g == len(groups) - 1
                if last and pe_t:
                    pe_t(e, b + 1, 0)
                    pe_t(e, b + 1, 1)
                for k in range(DK):
                    if g == 0:
                        ge(e, lo_sem, b * DK + k + 1)
                    for c, ch in enumerate(chunks):
                        if k == 0:
                            wait_bank(g, c)
                            if slot_ready:
                                slot_ready(ch)
                        s = slot_of(ch)
                        wh, wl = slot_hi(s)[:, k * P:(k + 1) * P], slot_lo(s)[:, k * P:(k + 1) * P]
                        m = parts3(e, PS[:, 3 * (g % 2) + c, :], wh, wl, zhi[:, k, :], zlo[:, k, :], k == 0, k == DK - 1)
                        if k == DK - 1:
                            inc(m, done)
                    if last and free and k < DK - 1:
                        inc(m, free)
                    if last and pe_t and k >= 2:
                        pe_t(e, b + 1, k)
                if after_group:
                    after_group(g)

        f_ld = [sem(f"fold_load{t}") for t in range(LC + 1)]
        f_t, f_xhi, f_xlo, f_hi, f_lo, f_mm, f_ev, f_st = (sem(f"fold_{n}") for n in (
            "transposed", "expert_hi", "expert_lo", "fc2_hi", "fc2_lo", "product", "staged", "stored"))
        ex_raw = SF[:, 0:LC * L].rearrange("p (t m) -> p t m", t=LC)
        f2_raw = SF[:, LC * L:LC * L + LC * D]
        exT = [mmf(i * LC * L, LC * L).rearrange("p (t l) -> p t l", t=LC) for i in range(2)]
        f2 = [mmf(2 * LC * L + i * LC * D, LC * D).rearrange("p (t n) -> p t n", t=LC) for i in range(2)]
        fold_out = f2_raw

        def fold_sp(e):
            inc(e.dma_start(ex_raw, expert_w.rearrange("(t p) m -> p t m", p=P)), f_ld[LC], 16)
            for t in range(LC):
                inc(e.dma_start(f2_raw[:, t * D:(t + 1) * D], fc2_w[t * P:(t + 1) * P, :]), f_ld[t], 16)
            ge(e, f_t, 1)

        def fold_store(e):
            ge(e, f_ev, 1)
            inc(e.dma_start(w_d.rearrange("(t p) n -> p t n", p=P), fold_out.rearrange("p (t n) -> p t n", t=LC)), f_st, 16)
            ge(e, f_st, 16)

        def fold_pe(e):
            ge(e, f_ld[LC], 16)
            ge(e, ph_start, 2)
            for mt in range(LC):
                for lt in range(LC):
                    m = e.transpose(PS[:, mt, lt * P:(lt + 1) * P], ex_raw[:, lt, mt * P:(mt + 1) * P], ident[:])
            inc(m, f_t)
            for mt in range(LC):
                if mt == 0:
                    ge(e, f_xlo, 1)
                ge(e, f_lo, mt + 1)
                for lt in range(LC):
                    for h in range(2):
                        lw = [t[:, mt, lt * P:(lt + 1) * P] for t in exT]
                        rv = [t[:, mt, h * NB:(h + 1) * NB] for t in f2]
                        m = parts3(e, PS[:, 2 * lt + h, :], lw[0], lw[1], rv[0], rv[1], mt == 0, mt == LC - 1)
            inc(m, f_mm)

        def fold_act(e):
            ge(e, f_ld[LC], 16)
            for t in range(LC + 1):
                if t == 1:
                    ge(e, f_t, 1)
                    inc(e.activation(exT[0], PS[:, 0:LC, :], ACT.Copy), f_xhi)
                c = t - 1 if t > 1 else t
                if t != 1:
                    ge(e, f_ld[c], 16)
                    inc(e.activation(f2[0][:, c, :], f2_raw[:, c * D:(c + 1) * D], ACT.Copy), f_hi)

        def fold_evac(e):
            ge(e, f_mm, 1)
            ge(e, f_lo, LC)
            inc(e.activation(fold_out, PS[:, :, :].rearrange("p b n -> p (b n)"), ACT.Copy), f_ev)

        def fold_dve(e):
            for t in range(LC):
                ge(e, f_hi, t + 1)
                inc(e.tensor_tensor(f2[1][:, t, :], f2_raw[:, t * D:(t + 1) * D], raw(f2[0][:, t, :]), ALU.subtract), f_lo)
                if t == 0:
                    ge(e, f_xhi, 1)
                    inc(e.tensor_tensor(exT[1], PS[:, 0:LC, :], raw(exT[0]), ALU.subtract), f_xlo)

        XN = SF[:, 0:ST * D].rearrange("p (t d) -> p t d", t=ST)
        wa_sp, wa_pe, wa_act, wa_dve, wa_lo, wa_tr = weight_prep(
            "wqkv", QC + 2 * KC, lambda j: wqkv[bass.ds(j * P, P), :], 0, 0)
        n_wa = QC + 2 * KC

        BC = B * C
        ctx_raw = SF[:, 4 * D:6 * D].rearrange("p (t d) -> p t d", t=2)
        cT = [mmf(Z0 + i * DK * BC, DK * BC).rearrange("p (k s) -> p k s", k=DK) for i in range(2)]
        STG = 4 * D
        stage = [SF[:, STG + c * NB:STG + (c + 1) * NB] for c in range(3)]
        vstage = [SF[:, STG + 3 * NB + t * KVE:STG + 3 * NB + (t + 1) * KVE] for t in range(2)]
        c_ld, c_t, c_hi, c_lo, c_mm, c_ev, c_st = (sem(f"ctx_{n}") for n in
                                                   ("load", "transposed", "hi", "lo", "product", "staged", "stored"))
        v_w = [MM[:, 15 * SLOT:18 * SLOT].rearrange("p (c h k e) -> p h k c e", c=KC, h=2, k=DK)[:, i] for i in range(2)]
        v_rows = v_d.rearrange("(q s) d -> q s d", s=T)
        k_b = k_d.rearrange("(b e) s -> e b s", b=B)

        def ctx_sp(e):
            inc(e.dma_start(ctx_raw, ctx.rearrange("(t b) s d -> (b s) t d", t=2)), c_ld, 16)

        def ctx_pe(e):
            ge(e, c_ld, 16)
            ge(e, wa_lo, n_wa)
            for k in range(DK):
                for t in range(2):
                    at = k * BC + t * P
                    m = e.transpose(PS[:, at // NB, at % NB:at % NB + P], ctx_raw[:, t, k * P:(k + 1) * P], ident[:])
            inc(m, c_t)
            ge(e, c_lo, 1)
            for c in range(KC):
                s = QC + c
                for k in range(DK):
                    wh, wl = slot_hi(s)[:, k * P:(k + 1) * P], slot_lo(s)[:, k * P:(k + 1) * P]
                    m = parts3(e, PS[:, 4 + c, 0:BC], wh, wl, cT[0][:, k, :], cT[1][:, k, :], k == 0, k == DK - 1)
                inc(m, c_mm)
            for t in range(2):
                for k in range(DK):
                    zt_ = [z[:, k, t * P:(t + 1) * P] for z in cT]
                    m = parts3(e, PS[:, t, 0:KVE], zt_[0], zt_[1], v_w[0][:, k], v_w[1][:, k], k == 0, k == DK - 1)
                inc(m, c_mm)

        def ctx_act(e):
            ge(e, c_t, 1)
            flat = PS[:, 0:4, :].rearrange("p b n -> p (b n)")
            inc(e.activation(mmf(Z0, DK * BC), flat, ACT.Copy), c_hi)
            a_sqrt(e, 0)
            for c in range(KC):
                ge(e, c_mm, c + 1)
                inc(e.activation(stage[c][:, 0:BC], PS[:, 4 + c, 0:BC], ACT.Copy), c_ev)
            for t in range(2):
                ge(e, c_mm, KC + t + 1)
                inc(e.activation(vstage[t], PS[:, t, 0:KVE], ACT.Copy), c_ev)
            for c in range(KC):
                ge(e, c_ev, KC + 2)
                inc(e.dma_start(k_b[c * P:(c + 1) * P, :, S:T], stage[c][:, 0:BC].rearrange("p (b s) -> p b s", b=B)), c_st, 16)
            for t in range(2):
                for h in range(2):
                    inc(e.dma_start(v_rows[(2 * t + h) * KV:(2 * t + h + 1) * KV, S:T, :].rearrange("h s d -> s h d"),
                                    vstage[t][h * C:(h + 1) * C, :].rearrange("p (h d) -> p h d", d=HD)), c_st, 16)
            ge(e, c_st, 16 * (KC + 4))

        def ctx_dve(e):
            ge(e, c_hi, 1)
            inc(e.tensor_tensor(mmf(Z0 + DK * BC, DK * BC), PS[:, 0:4, :].rearrange("p b n -> p (b n)"),
                                raw(mmf(Z0, DK * BC)), ALU.subtract), c_lo)

        a_acc = sem("a_product", 1)
        a_ev = sem("a_staged", 2)
        a_st = [sem(f"a_stored{c}", 16) for c in range(3)]
        a_vst = [sem(f"a_vstored{t}", 16) for t in range(2)]
        A_GROUPS = [[QC, QC + 1, QC + 2]] + [[3 * g, 3 * g + 1, 3 * g + 2] for g in range(QC // 3)]
        NQK = QC + KC
        A_EV = NQK + ST
        a_load, a_norm, a_sqrt, a_pet, a_hi, a_lo, a_zl, a_fr, a_zt = norm_z(
            "a", XN, lambda e, b: ge(e, a_acc, b * A_EV))

        def a_sp(e):
            hold(e, wa_tr, n_wa)
            with e.Fori(0, B) as b:
                a_load(e, x_r, b)

        def a_pe(e):
            def body(b, last):
                def wait_bank(g, c):
                    if g == 0:
                        if c < 2:
                            ge(e, a_ev, b * A_EV - 1 + c)
                    elif c == 0:
                        ge(e, a_ev, b * A_EV + 3 * max(g - 1, 0))

                mm_groups(e, b, A_GROUPS, a_zl, wait_bank, lambda ch: ch, a_acc)
                for t in range(ST):
                    g, c = t // 2, t % 2
                    if c == 0:
                        ge(e, a_ev, b * A_EV + 3 * (len(A_GROUPS) - 1 + g))
                    if t == ST - 2 and not last:
                        a_pet(e, b + 1, 0)
                        a_pet(e, b + 1, 1)
                    for k in range(DK):
                        zt_ = [z[:, k, t * P:(t + 1) * P] for z in (zhi, zlo)]
                        m = parts3(e, PS[:, 3 * ((g + 1) % 2) + c, 0:KVE], zt_[0], zt_[1],
                                   v_w[0][:, k], v_w[1][:, k], k == 0, k == DK - 1)
                        if k == DK - 1:
                            inc(m, a_acc)
                        elif t == ST - 1:
                            inc(m, a_fr)
                        if t == ST - 1 and k >= 2 and not last:
                            a_pet(e, b + 1, k)

            ge(e, c_ev, KC + 2)
            for k in range(DK):
                a_pet(e, 0, k)
            with e.Fori(0, B - 1) as b:
                body(b, False)
            body(B - 1, True)

        def a_act(e):
            def body(b, last):
                for g, chunks in enumerate(A_GROUPS):
                    for c, ch in enumerate(chunks):
                        n = 3 * g + c
                        ge(e, a_acc, b * A_EV + n + 1)
                        ge(e, a_st[c], b * (16 * len(A_GROUPS)) + 16 * g)
                        inc(e.activation(stage[c], PS[:, 3 * (g % 2) + c, :], ACT.Copy, scale=SCALE if ch < QC else 1.0), a_ev)
                        ge(e, a_ev, b * A_EV + n + 1)
                        if ch < QC:
                            dst = q_d[bass.ds(b * E + ch * P, P), :]
                        else:
                            dst = k_d[bass.ds(b * KVE + (ch - QC) * P, P), 0:S]
                        inc(e.dma_start(dst, stage[c]), a_st[c], 16)
                    if g == 2 and not last:
                        a_sqrt(e, b + 1)
                for t in range(ST):
                    if t == ST - 1 and not last:
                        for k in range(DK - 1):
                            a_hi(e, b + 1, k)
                    n = NQK + t
                    g, c = t // 2, t % 2
                    ge(e, a_acc, b * A_EV + n + 1)
                    ge(e, a_vst[c], b * (16 * (ST // 2)) + 16 * g)
                    inc(e.activation(vstage[c], PS[:, 3 * ((g + 1) % 2) + c, 0:KVE], ACT.Copy), a_ev)
                    ge(e, a_ev, b * A_EV + n + 1)
                    dst = v_rows[bass.ds(b * KV, KV), t * P:(t + 1) * P, :].rearrange("h s d -> s h d")
                    inc(e.dma_start(dst, vstage[c].rearrange("p (h d) -> p h d", d=HD)), a_vst[c], 16)
                if not last:
                    a_hi(e, b + 1, DK - 1)

            for k in range(DK):
                a_hi(e, 0, k)
            with e.Fori(0, B - 1) as b:
                body(b, False)
            body(B - 1, True)

        def a_dve(e):
            with e.Fori(0, B) as b:
                a_norm(e, b)
                for k in range(DK):
                    a_lo(e, b, k)

        def a_stored(e):
            for c in range(3):
                ge(e, a_st[c], 16 * B * len(A_GROUPS))
            for t in range(2):
                ge(e, a_vst[t], 16 * B * (ST // 2))

        WO0 = 6
        wo_v = wo.rearrange("(i p) e -> p i e", p=P)
        wb_sp, wb_pe, wb_act, wb_dve, wb_lo, wb_tr = weight_prep(
            "wo", QC, lambda j: wo_v[:, :, bass.ds(j * P, P)], WO0, 0)

        NG = B * KV
        NH = NG * G
        KB, VB, PB, QB = 0, 4 * T, 4608, Z0
        VW = HD
        kp = [[mmf(KB + p * 2 * T + i * T, T, HD) for i in range(2)] for p in range(2)]
        vp = [[mmf(VB + (2 * p + i) * NT * VW, NT * VW).rearrange("p (j d) -> p j d", j=NT) for i in range(2)] for p in range(2)]
        qp = [[mmf(QB + (2 * (1 - p) + i) * G * S, G * S, HD) for i in range(2)] for p in range(2)]
        pt = [[mmf(PB + (2 * j + i) * S, S) for i in range(2)] for j in range(NT)]
        assert VB + 4 * NT * VW <= PB and PB + 2 * NT * S <= WO0 * SLOT
        pu = [[SF[:, (hp * ST + u) * T:(hp * ST + u + 1) * T] for u in range(ST)] for hp in range(2)]
        OS0 = 2 * ST * T
        os_ = [SF[0:HD, OS0 + r * S:OS0 + (r + 1) * S] for r in range(2)]
        TH = T // 2
        su = [PS[:, 2 * i:2 * i + 2, :].rearrange("p b n -> p (b n)")[:, NB - TH:NB + TH] for i in range(2)]
        TB = [4, 5, 6, 4, 5]
        b_ld = [sem(f"b_loaded{p}") for p in range(2)]
        b_sp, b_S, b_T = sem("b_split"), sem("b_scores"), sem("b_transposed", 10)
        b_mx, b_ex, b_hi, b_lo = sem("b_max"), sem("b_exp", 2), sem("b_hi"), sem("b_lo", 5)
        b_pv, b_oe = sem("b_pv", 4), sem("b_o_left", 1)
        b_rc, b_nm, b_np = sem("b_recip"), sem("b_scaled"), sem("b_scaled_by_pool")
        b_os = [sem(f"b_o_stored{r}", 16) for r in range(2)]

        def b_loads(e, g, p):
            q = [
                e.dma_start(raw(kp[p][1]), k_d[bass.ds(g * HD, HD), :]),
                e.dma_start(raw(qp[p][1]).rearrange("p (h s) -> p h s", h=G),
                            q_d[bass.ds(g * (G * HD), G * HD), :].rearrange("(h p) s -> p h s", p=HD)),
                e.dma_start(raw(vp[p][1])[:, 0:ST, 0:HD], v_d[bass.ds(g * T, S), :].rearrange("(j p) d -> p j d", p=P)),
                e.dma_start(raw(vp[p][1])[0:C, ST, 0:HD], v_d[bass.ds(g * T + S, C), :]),
            ]
            for d in q:
                inc(d, b_ld[p], 16)

        def b_sp_eng(e):
            a_stored(e)
            b_loads(e, 0, 0)

            def body(i, last):
                for hh in range(2 * G):
                    n = i * (2 * G) + hh
                    p, a, r = hh // G, hh % G, hh % 2
                    if a == 0 and not (last and p == 1):
                        g = i * 2 + p
                        hold(e, b_pv, g * G)
                        b_loads(e, g + 1, 1 - p)
                    hold(e, b_oe, n + 1)
                    inc(e.dma_start(o_d[bass.ds(n * HD, HD), :], os_[r]), b_os[r], 16)
                    if last and hh == G - 1:
                        c_first_loads(e)

            with e.Fori(0, NG // 2 - 1) as i:
                body(i, False)
            body(NG // 2 - 1, True)

        PIECES = [[], ["k", "q0"], ["v", "q1"], ["q2", "q3"]]
        FIRST = ["k", "q0", "v", "q1", "q2", "q3"]

        def piece(nm, p):
            if nm == "k":
                return [(kp[p][0], kp[p][1])]
            if nm == "v":
                return [(vp[p][0][:, 0:ST, 0:HD], vp[p][1][:, 0:ST, 0:HD]), (vp[p][0][0:C, ST, 0:HD], vp[p][1][0:C, ST, 0:HD])]
            a = int(nm[1])
            return [tuple(t[:, a * S:(a + 1) * S] for t in qp[p])]

        def piece_hi(e, nm, p):
            for hi, lo in piece(nm, p):
                m = e.activation(hi, raw(lo), ACT.Copy)
            inc(m, b_ph)

        def piece_lo(e, nm, p, k):
            ge(e, b_ph, k + 1)
            for hi, lo in piece(nm, p):
                m = e.tensor_tensor(lo, raw(lo), raw(hi), ALU.subtract)
            inc(m, b_sp)

        def b_pool(e):
            def norm(m, mp, u):
                c = slice(mp * ST + u, mp * ST + u + 1)
                hold(e, b_rc, m * ST + u + 1)
                inc(e.tensor_scalar(pu[mp][u], pu[mp][u], rrec[:, c], None, ALU.mult), b_np)

            for k, nm in enumerate(FIRST):
                piece_lo(e, nm, 0, k)
            for u in range(2):
                norm(0, 0, u)

            def body(i, last):
                for hh in range(2 * G):
                    n = i * (2 * G) + hh
                    p, a = hh // G, hh % G
                    nx = not (last and hh == 2 * G - 1)
                    todo = [] if last and p == 1 else PIECES[a]
                    done = (i * 2 + p + 1) * 6 + sum(len(q) for q in PIECES[:a])
                    for u in range(2 if nx else 0):
                        norm(n + 1, (hh + 1) % 2, u)
                    for k, nm in enumerate(todo):
                        piece_lo(e, nm, 1 - p, done + k)

            with e.Fori(0, NG // 2 - 1) as i:
                body(i, False)
            body(NG // 2 - 1, True)

        b_ph = sem("b_pool_hi")

        def b_pe(e):
            def scores(m, p, a, u):
                if u == 0:
                    ge(e, b_sp, six(m, a) + [2, 4, 5, 6][a])
                ge(e, b_ex, m * ST + u - 1)
                qh, ql = (t[:, a * S + u * P:a * S + (u + 1) * P] for t in qp[p])
                parts3(e, su[u % 2][:, 0:TH], qh, ql, kp[p][0][:, 0:TH], kp[p][1][:, 0:TH], True, True)
                inc(parts3(e, su[u % 2][:, TH:T], qh, ql, kp[p][0][:, TH:T], kp[p][1][:, TH:T], True, True), b_S)

            def transp(n, hp, j):
                if j == 0:
                    ge(e, b_np, n * 2 + 2)
                    ge(e, b_nm, n * 2 + 2)
                if j != 2:
                    wait = hold if j == ST else ge
                    wait(e, b_lo, n * NT + [-1, 0, 0, 1, 2][j])
                w = P if j < ST else C
                for u in range(ST):
                    m = e.transpose(PS[0:w, TB[j], u * P:(u + 1) * P], pu[hp][u][:, j * P:j * P + w], ident[:])
                inc(m, b_T)

            def pv(n, p, a, j):
                if j == 0:
                    ge(e, b_oe, n)
                    if a == 0:
                        ge(e, b_sp, six(n, a) + 3)
                ge(e, b_lo, n * NT + j + 1)
                w = P if j < ST else C
                vh, vl = (t[0:w, j, :] for t in vp[p])
                ph, pl = (t[0:w, :] for t in pt[j])
                m = parts3(e, PS[0:HD, 7, :], vh, vl, ph, pl, j == 0, j == NT - 1)
                if j == NT - 1:
                    inc(m, b_pv)

            cur = [0, 0]

            def six(m, a):
                return cur[1]

            def body(i, last):
                for hh in range(2 * G):
                    n = i * (2 * G) + hh
                    p, a = hh // G, hh % G
                    nx = None if (last and hh == 2 * G - 1) else n + 1
                    pn, an = ((hh + 1) // G) % 2, (hh + 1) % G
                    gn = i * 2 + (hh + 1) // G

                    def s(u):
                        if nx is not None:
                            cur[1] = gn * 6
                            scores(nx, pn, an, u)

                    def v(j):
                        cur[1] = (i * 2 + p) * 6
                        pv(n, p, a, j)

                    hp = hh % 2
                    for step in ("s0", "t0", "s1", "t1", "t2", "s2", "t3", "v0", "t4", "s3", "v1", "v2", "v3", "v4"):
                        q = int(step[1])
                        {"t": lambda: transp(n, hp, q), "s": lambda: s(q), "v": lambda: v(q)}[step[0]]()

            ge(e, wb_lo, QC)
            cur[1] = 0
            for u in range(ST):
                scores(0, 0, 0, u)
            with e.Fori(0, NG // 2 - 1) as i:
                body(i, False)
            body(NG // 2 - 1, True)

        def b_act(e):
            def exps(m, mp, u):
                if u == 0:
                    ge(e, b_T, (m - 1) * NT)
                ge(e, b_mx, m * ST + u + 1)
                inc(e.activation(pu[mp][u], su[u % 2][:, 0:T], ACT.Exp, bias=negmax[:, mp * ST + u:mp * ST + u + 1],
                                 accum_out=rsum[:, mp * ST + u:mp * ST + u + 1]), b_ex)

            def hi(n, j):
                ge(e, b_T, n * NT + j + 1)
                if j == 0:
                    ge(e, b_pv, n)
                w = P if j < ST else C
                inc(e.activation(pt[j][0][0:w, :], PS[0:w, TB[j], :], ACT.Copy), b_hi)

            def body(i, last):
                for hh in range(2 * G):
                    n = i * (2 * G) + hh
                    r = hh % 2
                    p, a = hh // G, hh % G
                    nx = not (last and hh == 2 * G - 1)
                    todo = [] if last and p == 1 else PIECES[a]
                    for step in ("h0", "e0", "h1", "h2", "e1", "h3", "c0", "h4", "e2", "e3"):
                        q = int(step[1])
                        if step[0] == "h":
                            hi(n, q)
                        elif step[0] == "e" and nx:
                            exps(n + 1, (hh + 1) % 2, q)
                        elif step[0] == "c" and todo:
                            if a == 1:
                                ge(e, b_ld[1 - p], (i + 1 + p) * 64)
                            piece_hi(e, todo[0], 1 - p)
                    ge(e, b_pv, n + 1)
                    ge(e, b_os[r], i * (16 * G) + 16 * (hh // 2))
                    inc(e.activation(os_[r], PS[0:HD, 7, :], ACT.Copy), b_oe)
                    for nm in todo[1:]:
                        piece_hi(e, nm, 1 - p)

            ge(e, b_ld[0], 64)
            for nm in FIRST:
                piece_hi(e, nm, 0)
            for u in range(ST):
                exps(0, 0, u)
            with e.Fori(0, NG // 2 - 1) as i:
                body(i, False)
            body(NG // 2 - 1, True)

        def b_dve(e):
            def mx(m, mp, u):
                ge(e, b_S, m * ST + u + 1)
                inc(e.tensor_reduce(negmax[:, mp * ST + u:mp * ST + u + 1], su[u % 2][:, 0:T], AX.X, ALU.max, negate=True), b_mx)

            def recip(m, mp, u):
                c = slice(mp * ST + u, mp * ST + u + 1)
                ge(e, b_ex, m * ST + u + 1)
                inc(e.reciprocal(rrec[:, c], rsum[:, c]), b_rc)

            def norm(m, mp, u):
                c = slice(mp * ST + u, mp * ST + u + 1)
                ge(e, b_rc, m * ST + u + 1)
                inc(e.tensor_scalar(pu[mp][u], pu[mp][u], rrec[:, c], None, ALU.mult), b_nm)

            def lo(n, j):
                ge(e, b_hi, n * NT + j + 1)
                w = P if j < ST else C
                inc(e.tensor_tensor(pt[j][1][0:w, :], PS[0:w, TB[j], :], raw(pt[j][0][0:w, :]), ALU.subtract), b_lo)

            def body(i, last):
                for hh in range(2 * G):
                    n = i * (2 * G) + hh
                    nx = not (last and hh == 2 * G - 1)
                    mp = (hh + 1) % 2
                    for step in ("m0", "l0", "m1", "l1", "r0", "l2", "m2", "r1", "l3", "m3", "l4", "r2", "n2", "r3", "n3"):
                        q = int(step[1])
                        if step[0] == "l":
                            lo(n, q)
                        elif nx:
                            {"m": mx, "r": recip, "n": norm}[step[0]](n + 1, mp, q)

            for u in range(ST):
                mx(0, 0, u)
                recip(0, 0, u)
            for u in (2, 3):
                norm(0, 0, u)
            with e.Fori(0, NG // 2 - 1) as i:
                body(i, False)
            body(NG // 2 - 1, True)

        halves = [SF[:, h * NB:(h + 1) * NB] for h in range(2)]
        j_ld = [sem(f"job_raw{h}") for h in range(2)]
        j_hi, j_lo = sem("job_hi"), sem("job_lo", 2)
        up_v = up_w.rearrange("(k p) n -> p k n", p=P)
        fc_v = fc1_w.rearrange("(k p) n -> p k n", p=P)

        def job_src(j, h):
            kind, c = j
            if kind == "e":
                w, c = (down_w, c) if c < FC else (w_d, c - FC)
                return w[c * P:(c + 1) * P, h * NB:(h + 1) * NB]
            return (up_v if kind == "u" else fc_v)[:, h * (DK // 2):(h + 1) * (DK // 2), c * P:(c + 1) * P]

        def job_slot(j):
            return FC + j[1] % 2 if j[0] == "f" else j[1]

        def job_load(e, j, m):
            for h in range(2):
                src = job_src(j, h)
                hold(e, j_lo, m * 2 + h - 1)
                o = halves[h] if len(src.shape) == 2 else halves[h].rearrange("p (k e) -> p k e", k=DK // 2)
                inc(e.dma_start(o, src), j_ld[h], 16)

        def job_part(j, h, part):
            return part(job_slot(j))[:, h * NB:(h + 1) * NB]

        def job_hi(e, j, m, free=None):
            if free:
                free()
            for h in range(2):
                ge(e, j_ld[h], m * 16 + 16)
                inc(e.activation(job_part(j, h, slot_hi), halves[h], ACT.Copy), j_hi)

        def job_lo(e, j, m, done):
            for h in range(2):
                ge(e, j_hi, m * 2 + h + 1)
                inc(e.tensor_tensor(job_part(j, h, slot_lo), halves[h], raw(job_part(j, h, slot_hi)), ALU.subtract), j_lo)
            ge(e, j_lo, m * 2 + 2)
            e.sem_inc(sems[done][0], 1)

        D_GROUPS = [[("u", 0), ("u", 1), ("u", 2)], [("u", 3), ("u", 4), ("u", 5)], [("f", 0), ("u", 6), ("u", 7)],
                    [("f", 1), ("u", 8), ("u", 9)], [("f", 2), ("u", 10), ("u", 11)], [("u", 12), ("u", 13)],
                    [("f", 3), ("u", 14), ("u", 15)]]
        JOBS_C = {0: [("u", 0), ("u", 1)], 1: [("u", 2), ("u", 3)], 2: [("u", 4)], 3: [("u", 5)]}
        JOBS_FIRST = {-1: D_GROUPS[2], 0: D_GROUPS[3], 1: [("u", 10), ("u", 11)], 2: [("f", 2), ("u", 12), ("u", 13)],
                      3: D_GROUPS[6], 4: [("f", 0)]}
        JOBS_MID = {-1: [("f", 1)], 2: [("f", 2)], 3: [("f", 3)], 4: [("f", 0)]}
        JOBS_LAST = {-1: [("f", 1)], 0: [("e", 0), ("e", 1), ("e", 2)], 1: [("e", 3), ("e", 4), ("e", 5)],
                     2: [("f", 2), ("e", 6), ("e", 7)], 3: [("f", 3), ("e", 8), ("e", 9)], 4: [("e", 10), ("e", 11)],
                     5: [("e", 12), ("e", 13)], 6: [("e", 14), ("e", 15)]}

        def flat(jobs):
            return [(at, j) for at in sorted(jobs) for j in jobs[at]]

        N_C = len(flat(JOBS_C))
        N_FIRST = len(flat(JOBS_FIRST))
        N_MID = len(flat(JOBS_MID))
        N_LAST = len(flat(JOBS_LAST))
        M_FIRST = N_C
        M_MID = M_FIRST + N_FIRST
        M_LAST = M_MID + N_MID * (B - 2)
        M_E = M_LAST + N_LAST
        d_up, d_fc, e_sl = sem("d_up_slots"), sem("d_fc_slots"), sem("e_slots")
        DONE = {"u": d_up, "f": d_fc, "e": e_sl}

        CU = QC // 4
        CUB = Z0 + 2 * DK * S - 8 * CU * P
        cu = [[mmf(CUB + (2 * u + i) * CU * P, CU * P).rearrange("p (c s) -> p c s", c=CU) for i in range(2)] for u in range(4)]
        assert CUB >= QB + 2 * G * S
        XR = SF[:, 5 * D:6 * D]
        XN2 = SF[:, D:D + ST * D].rearrange("p (t d) -> p t d", t=ST)
        cc_ld = [sem(f"c_o_loaded{u}") for u in range(4)]
        cc_xl = sem("c_x_loaded")
        cc_hi, cc_lo = sem("c_o_hi"), sem("c_o_lo")
        cc_use, cc_x1 = sem("c_unit_used", 4), sem("c_x1", 2)
        cc_st = sem("c_stored")
        d_acc = sem("d_product", 20)

        d_load, d_norm, d_sqrt, d_pet0, d_hi, d_lo, d_zl, d_fr, d_zt = norm_z(
            "d", XN2, lambda e, b: ge(e, d_acc, b * ND))

        def c_load_unit(e, b, t, u):
            n = b * ST + t
            hold(e, cc_use, n * 4 + u - 3)
            src = o_d[bass.ds(b * E + u * CU * P, CU * P), t * P:(t + 1) * P]
            inc(e.dma_start(raw(cu[u][1]), src.rearrange("(c p) s -> p c s", p=P)), cc_ld[u], 16)

        def c_first_loads(e):
            hold(e, b_pv, (NG - 1) * G)
            for r in range(2):
                ge(e, b_os[r], H // 2 * 16)
            for u in range(4):
                c_load_unit(e, 0, 0, u)

        def c_sp_eng(e):
            def load_x(n):
                inc(e.dma_start(XR, x_r[bass.ds(n * P, P), :]), cc_xl, 16)

            def tiles(b, t0, jobs=None):
                m = 0
                for r in range(2):
                    hold(e, b_os[r], b * (H // 2 * 16) + H // 2 * 16)
                for t in range(t0, ST):
                    n = b * ST + t
                    for u in range(4):
                        c_load_unit(e, b, t, u)
                    hold(e, cc_x1, n)
                    inc(e.dma_start(x1_d[bass.ds(n * P - P, P), :], XR), cc_st, 16)
                    hold(e, cc_st, n * 16)
                    load_x(n)
                    for j in (jobs or {}).get(t, []):
                        job_load(e, j, m)
                        m += 1

            hold(e, b_pv, NH)
            for r in range(2):
                ge(e, b_os[r], NH // 2 * 16)
            load_x(0)
            tiles(0, 1)
            with e.Fori(1, B - 1) as b:
                tiles(b, 0)
            d_load(e, x1_d, 0)
            tiles(B - 1, 0, JOBS_C)
            hold(e, cc_x1, B * ST)
            inc(e.dma_start(x1_d[(B * ST - 1) * P:B * ST * P, :], XR), cc_st, 16)
            ge(e, cc_st, B * ST * 16)

        def c_act(e):
            def tiles(b, jobs=None):
                m = 0
                for t in range(ST):
                    n = b * ST + t
                    for u in range(4):
                        ge(e, cc_ld[u], n * 16 + 16)
                        inc(e.activation(cu[u][0], raw(cu[u][1]), ACT.Copy), cc_hi)
                    for j in (jobs or {}).get(t, []):
                        job_hi(e, j, m)
                        m += 1

            with e.Fori(0, B - 1) as b:
                tiles(b)
            d_sqrt(e, 0)
            tiles(B - 1, JOBS_C)
            for k in range(DK):
                d_hi(e, 0, k)

        def c_pool(e):
            def tiles(b, jobs=None):
                m = 0
                for t in range(ST):
                    n = b * ST + t
                    for u in range(4):
                        ge(e, cc_hi, n * 4 + u + 1)
                        inc(e.tensor_tensor(cu[u][1], raw(cu[u][1]), raw(cu[u][0]), ALU.subtract), cc_lo)
                    for j in (jobs or {}).get(t, []):
                        job_lo(e, j, m, DONE[j[0]])
                        m += 1

            with e.Fori(0, B - 1) as b:
                tiles(b)
            tiles(B - 1, JOBS_C)

        def units_under(k):
            over = Z0 + DK * S + (k + 1) * S - CUB
            return 0 if over <= 0 else -(-over // (2 * CU * P))

        def c_pe(e):
            at = {0: [0, 1], 2: [2], 4: [3], 8: [4], 9: [5], 11: [6]}

            def tile(b, t, transposes=False):
                n = b * ST + t
                ge(e, cc_x1, n - 1)
                for k in range(QC):
                    u, c = k // CU, k % CU
                    if transposes:
                        for q in at.get(k, []):
                            d_pet0(e, 0, q)
                    if c == 0:
                        ge(e, cc_lo, n * 4 + u + 1)
                    wh, wl = slot_hi(WO0 + k), slot_lo(WO0 + k)
                    for h in range(2):
                        hs = slice(h * NB, (h + 1) * NB)
                        m = parts3(e, PS[:, 2 * (t % 2) + h, :], cu[u][0][:, c, :], cu[u][1][:, c, :],
                                   wh[:, hs], wl[:, hs], k == 0, k == QC - 1)
                    if c == CU - 1:
                        inc(m, cc_use)

            ge(e, b_ex, NH * ST)
            with e.Fori(0, B - 1) as b:
                for t in range(ST):
                    tile(b, t)
            for t in range(ST):
                tile(B - 1, t, t == ST - 1)
            d_pet0(e, 0, DK - 1)

        def c_dve(e):
            def tile(b, t):
                n, r = b * ST + t, t % 2
                ge(e, cc_use, n * 4 + 4)
                ge(e, cc_xl, n * 16 + 16)
                inc(e.tensor_tensor(XR, PS[:, 2 * r:2 * r + 2, :].rearrange("p b n -> p (b n)"), XR, ALU.add), cc_x1)

            with e.Fori(0, B - 1) as b:
                for t in range(ST):
                    tile(b, t)
            d_norm(e, 0)
            for t in range(ST - 1):
                tile(B - 1, t)
            for k in range(DK):
                if k == DK - 2:
                    tile(B - 1, ST - 1)
                if units_under(k):
                    ge(e, cc_use, (B * ST - 1) * 4 + units_under(k))
                d_lo(e, 0, k)

        st2 = [SF[:, 5 * D + c * NB:5 * D + (c + 1) * NB] for c in range(3)]
        D_ALL = [c for g in D_GROUPS for c in g]
        D_CUM = [sum(len(x) for x in D_GROUPS[:g + 1]) for g in range(len(D_GROUPS))]
        ND = len(D_ALL)
        assert ND == FC + LC == 20 and FC == 16 and LC == 4
        d_ev, d_sq = sem("d_staged", 3), sem("d_squared")
        d_st = [sem(f"d_stored{c}", 16) for c in range(3)]
        D_USES = [sum(len(x) > c for x in D_GROUPS) for c in range(3)]
        d_gm, d_gc = sem("d_gate_product"), sem("d_gate_chain", 1)
        d_gw = sem("d_gate_weights")
        d_gl, d_gt = sem("d_gate_staged"), sem("d_gate_transposed")
        gTs = sm[:, 216:216 + P]
        gT = [gTs[32 * t:32 * t + 2 * NE, :] for t in range(ST)]
        GC = 7

        def jobs_of(b):
            if isinstance(b, int):
                return (JOBS_FIRST, M_FIRST) if b == 0 else (JOBS_LAST, M_LAST)
            return JOBS_MID, b * N_MID + (M_MID - N_MID)

        def d_sp_eng(e):
            for b in (0, None, B - 1):
                def run(b, n_before):
                    for m, (at, j) in enumerate(flat(jobs_of(b)[0])):
                        job_load(e, j, n_before + m)

                if b is not None:
                    run(b, jobs_of(b)[1])
                else:
                    with e.Fori(1, B - 1) as r:
                        run(r, jobs_of(r)[1])

        def d_pool(e):
            for b in (0, None, B - 1):
                def run(b, n_before):
                    for m, (at, j) in enumerate(flat(jobs_of(b)[0])):
                        job_lo(e, j, n_before + m, DONE[j[0]])

                if b is not None:
                    run(b, jobs_of(b)[1])
                else:
                    with e.Fori(1, B - 1) as r:
                        run(r, jobs_of(r)[1])

        def d_pe(e):
            def pet(e, b, k):
                if k == 0:
                    ge(e, d_gc, b * GC)
                d_pet0(e, b, k)

            def body(b, last):
                def wait_bank(g, c):
                    if g == 0:
                        ge(e, d_ev, b * ND - 2 + c)
                    elif c == 0:
                        ge(e, d_ev, b * ND + (D_CUM[g - 2] if g >= 2 else 0))

                def slot_ready(ch):
                    if ch[0] == "u":
                        ge(e, d_up, ch[1] + 1)
                    else:
                        ge(e, d_fc, b * LC + ch[1] + 1)

                def gate(g):
                    if g == 0:
                        ge(e, d_gw, 18)
                        for k in range(DK):
                            e.matmul(PS[0:2 * NE, 6, :], GW[:, k, :], zhi[:, k, :], start=k == 0, stop=False)
                            m = e.matmul(PS[0:2 * NE, 6, :], GW[:, k, :], zlo[:, k, :], start=False, stop=k == DK - 1)
                        inc(m, d_gm)
                    if g == 1:
                        hold(e, d_gl, b + 1)
                        inc(e.transpose(PS[:, 6, 0:P], gTs, ident[:]), d_gt)

                mm_groups(e, b, D_GROUPS, d_zl, wait_bank, job_slot, d_acc, slot_ready, gate, d_fr, None if last else pet)

            ge(e, cc_x1, B * ST)
            with e.Fori(0, B - 1) as b:
                body(b, False)
            body(B - 1, True)

        def d_act(e):
            def body(b, last):
                jobs, m0 = jobs_of(b)
                m = [0]

                def run(at, b):
                    for j in jobs.get(at, []):
                        done_before = {("f", 0): (0, 4), ("f", 1): (-1, 6), ("f", 2): (0, 2), ("f", 3): (0, 3)}
                        free = None
                        if j[0] == "e":
                            free = lambda: ge(e, d_acc, b * ND + D_ALL.index(("u", j[1])) + 1)
                        elif j[0] == "f" and not (isinstance(b, int) and b == 0 and at <= 0):
                            db, g = done_before[j]
                            free = lambda: ge(e, d_acc, (b + db) * ND + D_CUM[g])
                        elif at == -1:
                            free = lambda: ge(e, cc_use, B * ST * 4)
                        job_hi(e, j, m0 + m[0], free)
                        m[0] += 1

                run(-1, b)
                n, sq = 0, 0
                for g, chunks in enumerate(D_GROUPS):
                    if g == len(D_GROUPS) - 1 and not last:
                        for k in range(DK - 1):
                            d_hi(e, b + 1, k)
                    for c, ch in enumerate(chunks):
                        ge(e, d_acc, b * ND + n + c + 1)
                        ge(e, d_st[c], b * (16 * D_USES[c]) + 16 * sum(len(x) > c for x in D_GROUPS[:g]))
                        inc(e.activation(st2[c], PS[:, 3 * (g % 2) + c, :], ACT.Relu if ch[0] == "u" else ACT.Copy), d_ev)
                    if g == len(D_GROUPS) - 1 and not last:
                        d_hi(e, b + 1, DK - 1)
                    for c, ch in enumerate(chunks):
                        up = ch[0] == "u"
                        if up:
                            sq += 1
                            ge(e, d_sq, b * FC + sq)
                        else:
                            ge(e, d_ev, b * ND + n + 1)
                        row = ch[1] * P if up else F + ch[1] * P
                        inc(e.dma_start(h_d[bass.ds(b * (F + L) + row, P), :], st2[c]), d_st[c], 16)
                        n += 1
                    run(g, b)
                    if g == 0 and not last:
                        d_load(e, x1_d, b + 1)
                    if g == 2 and not last:
                        d_sqrt(e, b + 1)

            body(0, False)
            with e.Fori(1, B - 1) as b:
                body(b, False)
            body(B - 1, True)
            for c in range(3):
                ge(e, d_st[c], B * (16 * D_USES[c]))

        def d_dve(e):
            def body(b, last):
                n = 0
                for g, chunks in enumerate(D_GROUPS):
                    final = g == len(D_GROUPS) - 1 and not last
                    for k in range(DK - 1 if final else 0):
                        d_lo(e, b + 1, k)
                    for c, ch in enumerate(chunks):
                        if ch[0] == "u":
                            ge(e, d_ev, b * ND + n + 1)
                            inc(e.tensor_tensor(st2[c], st2[c], st2[c], ALU.mult), d_sq)
                        n += 1
                    if final:
                        d_lo(e, b + 1, DK - 1)
                    if g == 0:
                        hold(e, d_gm, b + 1)
                        for t in range(ST):
                            m = e.tensor_copy(gT[t], PS[0:2 * NE, 6, t * P:(t + 1) * P])
                        inc(m, d_gl)
                    if g == 1:
                        hold(e, d_gt, b + 1)
                        q = [0]

                        def link(ins):
                            q[0] += 1
                            inc(ins, d_gc)
                            hold(e, d_gc, b * GC + q[0])

                        link(e.tensor_copy(gsum, PS[:, 6, 0:P].rearrange("p (t e) -> p t e", t=ST)[:, :, 0:2 * NE]))
                        link(e.tensor_tensor(g8, gsum[:, :, 0:NE], gsum[:, :, NE:2 * NE], ALU.add))
                        for t in range(ST):
                            link(e.max(gtop[:, t, :], g8[:, t, :]))
                        link(e.tensor_tensor(rw[:, bass.ds(b * ST, ST)], gtop[:, :, 0], gtop[:, :, 1], ALU.add))
                        assert q[0] == GC
                    if g == 2 and not last:
                        d_norm(e, b + 1)

            ge(e, d_gw, 16)
            inc(e.tensor_copy(GW[:, :, 0:NE], graw), d_gw)
            ge(e, d_gw, 17)
            inc(e.tensor_tensor(GW[:, :, NE:2 * NE], graw, raw(GW[:, :, 0:NE]), ALU.subtract), d_gw)
            ge(e, d_gw, 18)
            inc(e.memset(gTs, 0.0), d_gw)
            ge(e, d_gw, 19)
            with e.Fori(0, B - 1) as b:
                body(b, False)
            body(B - 1, True)

        NK = FC + LC
        EU = NK // 4
        H0 = NK * SLOT
        eu = [[mmf(H0 + (2 * u + i) * EU * P, EU * P).rearrange("p (c s) -> p c s", c=EU) for i in range(2)] for u in range(4)]
        x1b = SF[:, D:2 * D]
        yb = [SF[:, (2 + r) * D:(3 + r) * D] for r in range(2)]
        gam, bet = SF[:, 4 * D:5 * D], SF[:, 5 * D:6 * D]
        e_ld = [sem(f"e_h_loaded{u}") for u in range(4)]
        e_hi, e_lo, e_use = sem("e_h_hi"), sem("e_h_lo"), sem("e_unit_used", 4)
        e_y, e_add, e_sq, e_ch = sem("e_routed"), sem("e_added", 2), sem("e_sqrt"), sem("e_chain")
        e_post = sem("e_post", 1)
        e_gb, e_xl = sem("e_gamma_beta"), sem("e_x1_loaded")
        e_st = [sem(f"e_stored{r}", 16) for r in range(2)]
        E_CHAIN = 13

        def e_load(e, b, t, u):
            n = b * ST + t
            hold(e, e_use, n * 4 + u - 3)
            src = h_d[bass.ds(b * (F + L) + u * EU * P, EU * P), t * P:(t + 1) * P]
            inc(e.dma_start(raw(eu[u][1]), src.rearrange("(c p) s -> p c s", p=P)), e_ld[u], 16)

        def e_load_x1(e, n):
            hold(e, e_post, n)
            inc(e.dma_start(x1b, x1_d[bass.ds(n * P, P), :]), e_xl, 16)

        def e_sp_eng(e):
            for c in range(3):
                ge(e, d_st[c], B * (16 * D_USES[c]))
            hold(e, d_acc, B * ND)
            for u in range(4):
                e_load(e, 0, 0, u)
            for m in range(LC):
                job_load(e, ("e", FC + m), M_E + m)
            inc(e.dma_start(gam, gamma.partition_broadcast(P)), e_gb, 16)
            inc(e.dma_start(bet, beta.partition_broadcast(P)), e_gb, 16)
            e_load_x1(e, 0)

            def rest(b, t0):
                for t in range(t0, ST):
                    for u in range(4):
                        e_load(e, b, t, u)
                    e_load_x1(e, b * ST + t)

            rest(0, 1)
            with e.Fori(1, B) as b:
                rest(b, 0)

        def e_pool(e):
            def split(n, u):
                ge(e, e_hi, n * 4 + u + 1)
                inc(e.tensor_tensor(eu[u][1], raw(eu[u][1]), raw(eu[u][0]), ALU.subtract), e_lo)

            for u in range(4):
                split(0, u)
            for m in range(LC):
                job_lo(e, ("e", FC + m), M_E + m, e_sl)
            for t in range(1, ST):
                for u in range(4):
                    split(t, u)
            with e.Fori(1, B) as b:
                for t in range(ST):
                    for u in range(4):
                        split(b * ST + t, u)

        def e_pe(e):
            ge(e, d_ev, B * ND)
            ge(e, d_gc, B * GC)
            with e.Fori(0, B) as b:
                for t in range(ST):
                    n = b * ST + t
                    ge(e, e_add, n - 1)
                    for k in range(NK):
                        u, c = k // EU, k % EU
                        if c == 0:
                            ge(e, e_lo, n * 4 + u + 1)
                        if t == 0:
                            ge(e, e_sl, k + 1)
                        wh, wl = slot_hi(k), slot_lo(k)
                        for h in range(2):
                            hs = slice(h * NB, (h + 1) * NB)
                            bank = 4 * (t % 2) + (0 if k < FC else 2) + h
                            m = parts3(e, PS[:, bank, :], eu[u][0][:, c, :], eu[u][1][:, c, :],
                                       wh[:, hs], wl[:, hs], k in (0, FC), k in (FC - 1, NK - 1))
                        if c == EU - 1:
                            inc(m, e_use)

        def bank2(i):
            return PS[:, i:i + 2, :].rearrange("p b n -> p (b n)")

        def e_act(e):
            def hi(n, u):
                ge(e, e_ld[u], n * 16 + 16)
                inc(e.activation(eu[u][0], raw(eu[u][1]), ACT.Copy), e_hi)

            def step(b, t, more):
                n, r = b * ST + t, t % 2
                if more:
                    for u in range(3):
                        hi(n + 1, u)
                ge(e, e_use, n * 4 + 4)
                ge(e, e_st[r], b * (16 * ST // 2) + 16 * (t // 2))
                inc(e.activation(yb[r], bank2(4 * r + 2), ACT.Copy, scale=rw[:, bass.ds(n, 1)]), e_y)
                if more:
                    hi(n + 1, 3)
                ge(e, e_ch, n * E_CHAIN + 6)
                inc(e.activation(rt[:, 0:1], rec[:, 0:1], ACT.Sqrt), e_sq)
                ge(e, e_post, n + 1)
                inc(e.dma_start(out_r[bass.ds(n * P, P), :], yb[r]), e_st[r], 16)

            for u in range(4):
                hi(0, u)
            for m in range(LC):
                job_hi(e, ("e", FC + m), M_E + m)
            with e.Fori(0, B - 1) as b:
                for t in range(ST):
                    step(b, t, True)
            for t in range(ST):
                step(B - 1, t, t < ST - 1)
            for r in range(2):
                ge(e, e_st[r], B * (16 * ST // 2))

        def e_dve(e):
            ge(e, e_gb, 32)
            with e.Fori(0, B) as b:
                for t in range(ST):
                    n, r = b * ST + t, t % 2
                    q = [0]

                    def link(ins, last=True):
                        q[0] += 1
                        inc(ins, e_ch)
                        if last:
                            hold(e, e_ch, n * E_CHAIN + q[0])

                    ge(e, e_y, n + 1)
                    inc(e.tensor_tensor(yb[r], bank2(4 * r), yb[r], ALU.add), e_add)
                    ge(e, e_add, n + 1)
                    for h in range(2):
                        link(e.bn_stats(stats[:, 0, h, :], yb[r][:, h * NB:(h + 1) * NB]), h == 1)
                    link(e.bn_aggr(mv[:, 0, :], stats[:, 0, :, :]))
                    link(e.tensor_scalar(ve[:, 0:1], mv[:, 0, 1:2], EPS, None, ALU.add))
                    link(e.reciprocal(rec[:, 0:1], ve[:, 0:1]))
                    link(e.tensor_scalar(rec[:, 1:2], ve[:, 0:1], -0.5, None, ALU.mult))
                    hold(e, e_sq, n + 1)
                    link(e.tensor_tensor(nt1[:, 0:1], rt[:, 0:1], rt[:, 0:1], ALU.mult))
                    link(e.tensor_tensor(nt1[:, 0:1], nt1[:, 0:1], rec[:, 1:2], ALU.mult))
                    link(e.tensor_scalar(nt1[:, 0:1], nt1[:, 0:1], 1.5, None, ALU.add))
                    link(e.tensor_tensor(rstd[:, 0:1], rt[:, 0:1], nt1[:, 0:1], ALU.mult))
                    link(e.tensor_scalar(yb[r], yb[r], mv[:, 0, 0:1], rstd[:, 0:1], ALU.subtract, ALU.mult))
                    link(e.tensor_tensor(yb[r], yb[r], gam, ALU.mult))
                    link(e.tensor_tensor(yb[r], yb[r], bet, ALU.add))
                    assert q[0] == E_CHAIN
                    ge(e, e_xl, n * 16 + 16)
                    inc(e.tensor_tensor(yb[r], yb[r], x1b, ALU.add), e_post)

        block = es.enter_context(nc.Block())

        @block.sync
        def _(e):
            fold_sp(e)
            fold_store(e)
            ctx_sp(e)
            wa_sp(e)
            a_sp(e)
            hold(e, a_zt, B * DK)
            inc(e.dma_start(graw, gate_w.rearrange("(k p) e -> p k e", p=P)), d_gw, 16)
            wb_sp(e)
            b_sp_eng(e)
            c_sp_eng(e)
            d_sp_eng(e)
            e_sp_eng(e)

        @block.gpsimd
        def _(e):
            for h, credit in sems.values():
                if credit:
                    e.sem_inc(h, credit)
            inc(e.memset(ident[:], 0.0), ph_start)
            ge(e, ph_start, 1)
            inc(e.affine_select(out=ident[:], in_=ident[:], compare_op=ALU.not_equal, fill=1.0, base=0,
                                pattern=[[-1, P]], channel_multiplier=1), ph_start)
            b_pool(e)
            c_pool(e)
            d_pool(e)
            e_pool(e)

        @block.scalar
        def _(e):
            fold_act(e)
            fold_evac(e)
            wa_act(e)
            ctx_act(e)
            a_act(e)
            wb_act(e)
            b_act(e)
            c_act(e)
            d_act(e)
            e_act(e)

        @block.vector
        def _(e):
            fold_dve(e)
            wa_dve(e)
            ctx_dve(e)
            a_dve(e)
            wb_dve(e)
            b_dve(e)
            c_dve(e)
            d_dve(e)
            e_dve(e)

        @block.tensor
        def _(e):
            fold_pe(e)
            ge(e, f_ev, 1)
            wa_pe(e)
            ctx_pe(e)
            a_pe(e)
            ge(e, a_ev, B * A_EV)
            wb_pe(e)
            b_pe(e)
            c_pe(e)
            d_pe(e)
            e_pe(e)


_P = "L0_xattn_"
_F = "L0_ffn_"


def kernel(**inputs):
    import numpy as np
    import concourse.bacc as bacc
    from concourse.bass_utils import run_bass_kernel_spmd

    arrays = {
        "x": inputs["x"],
        "ctx": inputs["ctx_4096"],
        "wqkv": np.concatenate([np.asarray(inputs[_P + w]) for w in ("Wq", "Wk", "Wv")], axis=0),
        "wo": inputs[_P + "Wo"],
        "gate_w": inputs[_F + "gate_w"],
        "up_w": inputs[_F + "up_w"],
        "down_w": inputs[_F + "down_w"],
        "fc1_w": inputs[_F + "fc1_w"],
        "fc2_w": inputs[_F + "fc2_w"],
        "expert_w": inputs[_F + "expert_w"],
        "gamma": inputs[_F + "ln_gamma"],
        "beta": inputs[_F + "ln_beta"],
    }
    arrays = {f"in_{k}": np.ascontiguousarray(v) for k, v in arrays.items()}
    nc = bacc.Bacc("TRN2", target_bir_lowering=False, num_devices=1)
    aps = [nc.dram_tensor(k, v.shape, mybir.dt.from_np(v.dtype), kind="ExternalInput").ap() for k, v in arrays.items()]
    out = nc.dram_tensor("out", arrays["in_x"].shape, mybir.dt.float32, kind="ExternalOutput").ap()
    xattn_ffn_kernel(nc, *aps, out)
    r = run_bass_kernel_spmd(nc, [arrays], core_ids=[0])
    return r.results[0]["out"]
```

```python
import concourse.bass as bass
from concourse import mybir
from contextlib import ExitStack


def xattn_ffn_kernel(nc, x, ctx, wqkv, wo, gate_w, up_w, down_w, fc1_w, fc2_w, expert_w, gamma, beta, out):
    f32 = mybir.dt.float32
    f32r = mybir.dt.float32r
    ALU = mybir.AluOpType
    ACT = mybir.ActivationFunctionType
    AX = mybir.AxisListType

    P = 128
    B, S, D = x.shape
    C = ctx.shape[1]
    T = S + C
    HD = 96
    E = wo.shape[1]
    H = E // HD
    KVE = (wqkv.shape[0] - E) // 2
    KV = KVE // HD
    G = H // KV
    F = up_w.shape[1]
    L = fc1_w.shape[1]
    NE = gate_w.shape[1]
    EPS = 1e-5
    SCALE = float(HD) ** -0.5

    DK = D // P
    ST = S // P
    NT = T // P + 1
    QC, KC = E // P, KVE // P
    FC, LC = F // P, L // P
    NB = S
    assert D == 1024 and S == 512 and C == 64 and NT == 5 and KC == 3 and QC == 12 and G == 4

    def dram(name, shape):
        return nc.dram_tensor(name, shape, f32, kind="Internal").ap()

    q_d = dram("q_scratch", (B * E, S))
    k_d = dram("k_scratch", (B * KVE, T))
    v_d = dram("v_scratch", (B * KV * T, HD))
    o_d = dram("o_scratch", (B * E, S))
    x1_d = dram("x1_scratch", (B * S, D))
    h_d = dram("h_scratch", (B * (F + L), S))
    w_d = dram("fold_scratch", (L, D))

    x_r = x.rearrange("b s d -> (b s) d")
    out_r = out.rearrange("b s d -> (b s) d")

    es = ExitStack()
    with es:
        SLOT = 2 * D
        MM = es.enter_context(nc.sbuf_tensor("operands", [P, 22 * SLOT + 1024], f32r))
        SF = es.enter_context(nc.sbuf_tensor("staging", [P, 6656], f32))
        ident = es.enter_context(nc.sbuf_tensor("ident", [P, P], f32))
        sm = es.enter_context(nc.sbuf_tensor("small", [P, 344], f32))
        PS = es.enter_context(nc.psum_tensor("psum", [P, 8, NB], f32))

        def mmf(a, n, p=P, p0=0):
            return MM[p0:p0 + p, a:a + n]

        def raw(ap):
            return ap.bitcast(f32)

        def slot_hi(s):
            return mmf(s * SLOT, D)

        def slot_lo(s):
            return mmf(s * SLOT + D, D)

        Z0 = 18 * SLOT
        zhi = mmf(Z0, DK * S).rearrange("p (k s) -> p k s", k=DK)
        zlo = mmf(Z0 + DK * S, DK * S).rearrange("p (k s) -> p k s", k=DK)

        GW = mmf(22 * SLOT, DK * 2 * NE).rearrange("p (k e) -> p k e", k=DK)

        stats = sm[:, 0:48].rearrange("p (t h s) -> p t h s", t=4, h=2)
        mv = sm[:, 48:56].rearrange("p (t s) -> p t s", t=4)
        ve, rec, rt, nt1, rstd = (sm[:, 56 + 4 * i:60 + 4 * i] for i in range(5))
        negmax = sm[:, 80:88]
        gsum = sm[:, 88:152].rearrange("p (t e) -> p t e", t=4)
        g8 = sm[:, 152:184].rearrange("p (t e) -> p t e", t=4)
        gtop = sm[:, 88:120].rearrange("p (t e) -> p t e", t=4)
        rw = sm[:, 184:200]
        rsum, rrec = sm[:, 296:304], sm[:, 304:312]
        graw = sm[:, 232:296].rearrange("p (k e) -> p k e", k=DK)

        sems = {}

        def sem(name, credit=0):
            s = es.enter_context(nc.semaphore(name))
            sems[name] = (s, credit)
            return name

        def ge(e, name, v):
            s, c = sems[name]
            e.wait_ge(s, v + c)

        def hold(e, name, v):
            ge(e, name, v)
            e.sem_inc(idle, 1)

        def inc(ins, name, n=1):
            ins.then_inc(sems[name][0], n)

        idle = es.enter_context(nc.semaphore("idle"))

        def parts3(e, o, lh, ll, rh, rl, first, last):
            e.matmul(o, lh, rh, start=first, stop=False)
            e.matmul(o, lh, rl, start=False, stop=False)
            return e.matmul(o, ll, rh, start=False, stop=last)

        ph_start = sem("constants_ready")

        def weight_prep(tag, n, src, slot0, raw_area, nb=3):
            ld = [sem(f"{tag}_raw{p}") for p in range(nb)]
            tr = sem(f"{tag}_transposed", nb)
            hi = sem(f"{tag}_hi")
            lo = sem(f"{tag}_lo", nb)
            rawb = [raw_area[:, p * D:(p + 1) * D] for p in range(nb)]
            bank = [PS[:, 2 * p:2 * p + 2, :].rearrange("p b n -> p (b n)") for p in range(nb)]
            assert n % nb == 0

            def dst(i, p, off):
                return MM[:, bass.ds(i * (nb * SLOT) + ((slot0 + p) * SLOT + off), D)]

            def rounds(step):
                def run(e, i0=0, i1=n // nb, before=None, after=None, at=None):
                    def body(i):
                        if before:
                            before(e, i)
                        for p in range(nb):
                            if at and (i, p) in at:
                                at[i, p]()
                            step(e, i, p)
                        if after:
                            after(e, i)

                    if before or after or i1 - i0 == 1:
                        for i in range(i0, i1):
                            body(i)
                    else:
                        with e.Fori(i0, i1) as i:
                            body(i)
                return run

            def sp(e, i, p):
                hold(e, tr, i * nb + p + 1 - nb)
                view = src(i * nb + p)
                o = rawb[p] if len(view.shape) == 2 else rawb[p].rearrange("p (i e) -> p i e", e=P)
                inc(e.dma_start(o, view), ld[p], 16)

            def pe(e, i, p):
                ge(e, ld[p], i * 16 + 16)
                ge(e, lo, i * nb + p + 1 - nb)
                for k in range(DK):
                    m = e.transpose(bank[p][:, k * P:(k + 1) * P], rawb[p][:, k * P:(k + 1) * P], ident[:])
                inc(m, tr)

            def act(e, i, p):
                ge(e, tr, i * nb + p + 1)
                inc(e.activation(dst(i, p, 0), bank[p], ACT.Copy), hi)

            def dve(e, i, p):
                ge(e, hi, i * nb + p + 1)
                inc(e.tensor_tensor(dst(i, p, D), bank[p], raw(dst(i, p, 0)), ALU.subtract), lo)

            return rounds(sp), rounds(pe), rounds(act), rounds(dve), lo, tr

        LN_CHAIN = 18

        def norm_z(tag, xn, last_free):
            ld = sem(f"{tag}_x")
            ch = sem(f"{tag}_chain")
            sq = sem(f"{tag}_sqrt")
            zn = sem(f"{tag}_z")
            zt = sem(f"{tag}_zt", 8)
            zh = sem(f"{tag}_zhi")
            zl = sem(f"{tag}_zlo", 8)
            fr = sem(f"{tag}_zfree", DK)

            def load(e, src, b):
                hold(e, zt, b * DK)
                inc(e.dma_start(xn, src[bass.ds(b * S, S), :].rearrange("(t p) d -> p t d", p=P)), ld, 16)

            def dve_norm(e, b):
                n = [0]

                def link(ins, last=True):
                    n[0] += 1
                    inc(ins, ch)
                    if last:
                        hold(e, ch, b * LN_CHAIN + n[0])

                hold(e, ld, b * 16 + 16)
                for t in range(ST):
                    for h in range(2):
                        link(e.bn_stats(stats[:, t, h, :], xn[:, t, h * NB:(h + 1) * NB]), (t, h) == (ST - 1, 1))
                for t in range(ST):
                    link(e.bn_aggr(mv[:, t, :], stats[:, t, :, :]), t == ST - 1)
                link(e.tensor_scalar(ve, mv[:, :, 1], EPS, None, ALU.add))
                link(e.reciprocal(rec, ve))
                hold(e, sq, b + 1)
                link(e.tensor_tensor(nt1, rt, rt, ALU.mult))
                link(e.tensor_tensor(nt1, nt1, ve, ALU.mult))
                link(e.tensor_scalar(nt1, nt1, -0.5, 1.5, ALU.mult, ALU.add))
                link(e.tensor_tensor(rstd, rt, nt1, ALU.mult))
                assert n[0] == LN_CHAIN
                for t in range(ST):
                    z = e.tensor_scalar(xn[:, t, :], xn[:, t, :], mv[:, t, 0:1], rstd[:, t:t + 1], ALU.subtract, ALU.mult)
                inc(z, zn)

            def act_sqrt(e, b):
                ge(e, ch, b * LN_CHAIN + 14)
                inc(e.activation(rt, rec, ACT.Sqrt), sq)

            def pe_t(e, b, k):
                if k == 0:
                    ge(e, zn, b + 1)
                ge(e, zl, b * DK + k - 1)
                for t in range(ST):
                    m = e.transpose(PS[:, 6 + k % 2, t * P:(t + 1) * P], xn[:, t, k * P:(k + 1) * P], ident[:])
                inc(m, zt)

            def act_hi(e, b, k):
                ge(e, zt, b * DK + k + 1)
                if k < DK - 1:
                    ge(e, fr, (b - 1) * (DK - 1) + k + 1)
                else:
                    last_free(e, b)
                inc(e.activation(zhi[:, k, :], PS[:, 6 + k % 2, :], ACT.Copy), zh)

            def dve_lo(e, b, k):
                ge(e, zh, b * DK + k + 1)
                inc(e.tensor_tensor(zlo[:, k, :], PS[:, 6 + k % 2, :], raw(zhi[:, k, :]), ALU.subtract), zl)

            return load, dve_norm, act_sqrt, pe_t, act_hi, dve_lo, zl, fr, zt

        def mm_groups(e, b, groups, lo_sem, wait_bank, slot_of, done, slot_ready=None, after_group=None, free=None, pe_t=None):
            for g, chunks in enumerate(groups):
                last = g == len(groups) - 1
                if last and pe_t:
                    pe_t(e, b + 1, 0)
                    pe_t(e, b + 1, 1)
                for k in range(DK):
                    if g == 0:
                        ge(e, lo_sem, b * DK + k + 1)
                    for c, ch in enumerate(chunks):
                        if k == 0:
                            wait_bank(g, c)
                            if slot_ready:
                                slot_ready(ch)
                        s = slot_of(ch)
                        wh, wl = slot_hi(s)[:, k * P:(k + 1) * P], slot_lo(s)[:, k * P:(k + 1) * P]
                        m = parts3(e, PS[:, 3 * (g % 2) + c, :], wh, wl, zhi[:, k, :], zlo[:, k, :], k == 0, k == DK - 1)
                        if k == DK - 1:
                            inc(m, done)
                    if last and free and k < DK - 1:
                        inc(m, free)
                    if last and pe_t and k >= 2:
                        pe_t(e, b + 1, k)
                if after_group:
                    after_group(g)

        XN = SF[:, 0:ST * D].rearrange("p (t d) -> p t d", t=ST)
        wa_sp, wa_pe, wa_act, wa_dve, wa_lo, wa_tr = weight_prep(
            "wqkv", QC + 2 * KC, lambda j: wqkv[bass.ds(j * P, P), :], 0, SF[:, 0:3 * D])
        n_wa = QC + 2 * KC
        NQ = 4
        FQ = D // NQ
        f_xld, f_ld = sem("fold_expert_load"), sem("fold_fc2_load")
        f_t, f_xhi, f_xlo, f_hi, f_mm = (sem(f"fold_{n}") for n in ("transposed", "expert_hi", "expert_lo", "fc2_hi", "product"))
        f_lo = sem("fold_fc2_lo", 1)
        f_ev, f_st = sem("fold_staged", 1), sem("fold_stored", 16)
        ex_raw = SF[:, 4 * D:4 * D + LC * L].rearrange("p (t m) -> p t m", t=LC)
        F0 = 12 * SLOT
        exT = [mmf(F0 + i * LC * L, LC * L).rearrange("p (t l) -> p t l", t=LC) for i in range(2)]
        f2 = [[mmf(F0 + 2 * LC * L + i * LC * D + q * LC * FQ, LC * FQ).rearrange("p (t n) -> p t n", t=LC)
               for q in range(NQ)] for i in range(2)]
        f2_raw = SF[:, 3 * D:4 * D].rearrange("p (t n) -> p t n", t=LC)
        f_out = SF[:, 4 * D:5 * D].rearrange("p (t n) -> p t n", t=LC)
        assert F0 + 2 * LC * L + 2 * LC * D <= 18 * SLOT and LC * FQ == 2 * NB

        def quarter(ap, i):
            return ap[:, :, i * FQ:(i + 1) * FQ]

        def f_load(e, i):
            hold(e, f_lo, i)
            inc(e.dma_start(f2_raw, quarter(fc2_w.rearrange("(t p) n -> p t n", p=P), i)), f_ld, 16)

        def f_expert(e):
            ge(e, f_xld, 16)
            ge(e, ph_start, 2)
            for mt in range(LC):
                for lt in range(LC):
                    m = e.transpose(PS[:, 4 + mt, lt * P:(lt + 1) * P], ex_raw[:, lt, mt * P:(mt + 1) * P], ident[:])
            inc(m, f_t)

        def f_product(e, i):
            ge(e, f_lo, i + 1)
            ge(e, f_ev, i)
            for lt in range(LC):
                o = PS[:, 6 + lt // 2, (lt % 2) * FQ:(lt % 2 + 1) * FQ]
                for mt in range(LC):
                    lw = [t[:, mt, lt * P:(lt + 1) * P] for t in exT]
                    rv = [t[i][:, mt, :] for t in f2]
                    m = parts3(e, o, lw[0], lw[1], rv[0], rv[1], mt == 0, mt == LC - 1)
            inc(m, f_mm)

        def f_fc2_hi(e, i):
            ge(e, f_ld, i * 16 + 16)
            inc(e.activation(f2[0][i], f2_raw, ACT.Copy), f_hi)

        def f_evac(e, i):
            ge(e, f_mm, i + 1)
            ge(e, f_st, i * 16)
            inc(e.activation(f_out, PS[:, 6:8, :].rearrange("p b (t n) -> p (b t) n", n=FQ), ACT.Copy), f_ev)
            ge(e, f_ev, i + 1)
            inc(e.dma_start(quarter(w_d.rearrange("(t p) n -> p t n", p=P), i), f_out), f_st, 16)

        def f_between(e, i):
            if i + 1 < NQ:
                f_fc2_hi(e, i + 1)
            f_evac(e, i)

        def f_pool(e):
            for i in range(NQ):
                ge(e, f_hi, i + 1)
                inc(e.tensor_tensor(f2[1][i], f2_raw, raw(f2[0][i]), ALU.subtract), f_lo)

        BC = B * C
        KH = DK // 2
        ctx_raw = [SF[:, 5 * D:6 * D], SF[:, 3 * D:4 * D]]
        cT = [mmf(Z0 + i * DK * BC, DK * BC).rearrange("p (k s) -> p k s", k=DK) for i in range(2)]
        STG = 4 * D
        stage = [SF[:, STG + c * NB:STG + (c + 1) * NB] for c in range(3)]
        vstage = [SF[:, STG + 3 * NB + t * KVE:STG + 3 * NB + (t + 1) * KVE] for t in range(2)]
        c_ld, c_t, c_hi, c_lo, c_mm, c_ev, c_st = (sem(f"ctx_{n}") for n in
                                                   ("load", "transposed", "hi", "lo", "product", "staged", "stored"))
        v_w = [MM[:, 15 * SLOT:18 * SLOT].rearrange("p (c h k e) -> p h k c e", c=KC, h=2, k=DK)[:, i] for i in range(2)]
        v_rows = v_d.rearrange("(q s) d -> q s d", s=T)
        k_b = k_d.rearrange("(b e) s -> e b s", b=B)
        c_bank = PS[:, 6:8, :].rearrange("p b (k s) -> p (b k) s", s=BC)

        def ctx_t(e, h):
            for k in range(KH):
                for t in range(2):
                    m = e.transpose(c_bank[:, k, t * P:(t + 1) * P], ctx_raw[t][:, (h * KH + k) * P:(h * KH + k + 1) * P], ident[:])
            inc(m, c_t)

        def ctx_hi(e, h):
            ge(e, c_t, h + 1)
            inc(e.activation(cT[0][:, h * KH:(h + 1) * KH, :], c_bank, ACT.Copy), c_hi)

        def ctx_lo(e, h):
            ge(e, c_hi, h + 1)
            inc(e.tensor_tensor(cT[1][:, h * KH:(h + 1) * KH, :], c_bank, raw(cT[0][:, h * KH:(h + 1) * KH, :]), ALU.subtract), c_lo)

        def p0_sp(e):
            inc(e.dma_start(ex_raw, expert_w.rearrange("(t p) m -> p t m", p=P)), f_xld, 16)
            wa_sp(e, 0, NQ, before=f_load)
            hold(e, f_lo, NQ)
            for t, o in enumerate(ctx_raw):
                inc(e.dma_start(o, ctx[t * (B // 2):(t + 1) * (B // 2)].rearrange("b s d -> (b s) d")), c_ld, 16)
            wa_sp(e, NQ, n_wa // 3)
            hold(e, wa_tr, n_wa)
            hold(e, c_t, 2)
            a_load(e, x_r, 0)

        def p0_pe(e):
            f_expert(e)
            wa_pe(e, 0, NQ, after=f_product, at={(0, 2): lambda: ge(e, f_xlo, 1)})
            ge(e, c_ld, 32)
            ge(e, f_ev, NQ)
            ctx_t(e, 0)
            wa_pe(e, NQ, n_wa // 3)
            ge(e, c_lo, 1)
            ctx_t(e, 1)
            for k in range(DK):
                if k == KH:
                    ge(e, c_lo, 2)
                for c in range(KC):
                    if k == 0:
                        ge(e, wa_lo, n_wa - 2 + c // 2)
                    s = QC + c
                    wh, wl = slot_hi(s)[:, k * P:(k + 1) * P], slot_lo(s)[:, k * P:(k + 1) * P]
                    m = parts3(e, PS[:, c, 0:BC], wh, wl, cT[0][:, k, :], cT[1][:, k, :], k == 0, k == DK - 1)
                    if k == DK - 1:
                        inc(m, c_mm)
            ge(e, wa_lo, n_wa)
            for t in range(2):
                for k in range(DK):
                    zt_ = [z[:, k, t * P:(t + 1) * P] for z in cT]
                    m = parts3(e, PS[:, 3 + t, 0:KVE], zt_[0], zt_[1], v_w[0][:, k], v_w[1][:, k], k == 0, k == DK - 1)
                inc(m, c_mm)

        def p0_act(e):
            ge(e, f_t, 1)
            inc(e.activation(exT[0], PS[:, 4:4 + LC, :], ACT.Copy), f_xhi)
            f_fc2_hi(e, 0)
            wa_act(e, 0, NQ, after=f_between)
            ctx_hi(e, 0)
            wa_act(e, NQ, n_wa // 3)
            ctx_hi(e, 1)
            ge(e, f_st, NQ * 16)
            for c in range(KC):
                ge(e, c_mm, c + 1)
                inc(e.activation(stage[c][:, 0:BC], PS[:, c, 0:BC], ACT.Copy), c_ev)
            for t in range(2):
                if t == 1:
                    a_sqrt(e, 0)
                ge(e, c_mm, KC + t + 1)
                inc(e.activation(vstage[t], PS[:, 3 + t, 0:KVE], ACT.Copy), c_ev)
            for c in range(KC):
                ge(e, c_ev, KC + 2)
                inc(e.dma_start(k_b[c * P:(c + 1) * P, :, S:T], stage[c][:, 0:BC].rearrange("p (b s) -> p b s", b=B)), c_st, 16)
            for t in range(2):
                for h in range(2):
                    inc(e.dma_start(v_rows[(2 * t + h) * KV:(2 * t + h + 1) * KV, S:T, :].rearrange("h s d -> s h d"),
                                    vstage[t][h * C:(h + 1) * C, :].rearrange("p (h d) -> p h d", d=HD)), c_st, 16)


        def p0_act_stored(e):
            ge(e, c_st, 16 * (KC + 4))

        def p0_dve(e):
            ge(e, f_xhi, 1)
            inc(e.tensor_tensor(exT[1], PS[:, 4:4 + LC, :], raw(exT[0]), ALU.subtract), f_xlo)
            wa_dve(e, 0, NQ)
            ctx_lo(e, 0)
            wa_dve(e, NQ, n_wa // 3)
            ctx_lo(e, 1)
            a_norm(e, 0)

        a_acc = sem("a_product", 1)
        a_ev = sem("a_staged", 2)
        a_st = [sem(f"a_stored{c}", 16) for c in range(3)]
        a_vst = [sem(f"a_vstored{t}", 16) for t in range(2)]
        A_GROUPS = [[QC, QC + 1, QC + 2]] + [[3 * g, 3 * g + 1, 3 * g + 2] for g in range(QC // 3)]
        NQK = QC + KC
        A_EV = NQK + ST
        a_load, a_norm, a_sqrt, a_pet, a_hi, a_lo, a_zl, a_fr, a_zt = norm_z(
            "a", XN, lambda e, b: ge(e, a_acc, b * A_EV))

        def a_sp(e):
            hold(e, wa_tr, n_wa)
            with e.Fori(1, B) as b:
                a_load(e, x_r, b)

        def a_pe(e):
            def body(b, last):
                def wait_bank(g, c):
                    if g == 0:
                        if c < 2:
                            ge(e, a_ev, b * A_EV - 1 + c)
                    elif c == 0:
                        ge(e, a_ev, b * A_EV + 3 * max(g - 1, 0))

                mm_groups(e, b, A_GROUPS, a_zl, wait_bank, lambda ch: ch, a_acc)
                for t in range(ST):
                    g, c = t // 2, t % 2
                    if c == 0:
                        ge(e, a_ev, b * A_EV + 3 * (len(A_GROUPS) - 1 + g))
                    if t == ST - 2 and not last:
                        a_pet(e, b + 1, 0)
                        a_pet(e, b + 1, 1)
                    for k in range(DK):
                        zt_ = [z[:, k, t * P:(t + 1) * P] for z in (zhi, zlo)]
                        m = parts3(e, PS[:, 3 * ((g + 1) % 2) + c, 0:KVE], zt_[0], zt_[1],
                                   v_w[0][:, k], v_w[1][:, k], k == 0, k == DK - 1)
                        if k == DK - 1:
                            inc(m, a_acc)
                        elif t == ST - 1:
                            inc(m, a_fr)
                        if t == ST - 1 and k >= 2 and not last:
                            a_pet(e, b + 1, k)

            ge(e, c_ev, KC + 2)
            for k in range(DK):
                a_pet(e, 0, k)
            with e.Fori(0, B - 1) as b:
                body(b, False)
            body(B - 1, True)

        def a_act(e):
            def body(b, last):
                for g, chunks in enumerate(A_GROUPS):
                    for c, ch in enumerate(chunks):
                        n = 3 * g + c
                        ge(e, a_acc, b * A_EV + n + 1)
                        ge(e, a_st[c], b * (16 * len(A_GROUPS)) + 16 * g)
                        inc(e.activation(stage[c], PS[:, 3 * (g % 2) + c, :], ACT.Copy, scale=SCALE if ch < QC else 1.0), a_ev)
                        ge(e, a_ev, b * A_EV + n + 1)
                        if ch < QC:
                            dst = q_d[bass.ds(b * E + ch * P, P), :]
                        else:
                            dst = k_d[bass.ds(b * KVE + (ch - QC) * P, P), 0:S]
                        inc(e.dma_start(dst, stage[c]), a_st[c], 16)
                    if g == 2 and not last:
                        a_sqrt(e, b + 1)
                for t in range(ST):
                    if t == ST - 1 and not last:
                        for k in range(DK - 1):
                            a_hi(e, b + 1, k)
                    n = NQK + t
                    g, c = t // 2, t % 2
                    ge(e, a_acc, b * A_EV + n + 1)
                    ge(e, a_vst[c], b * (16 * (ST // 2)) + 16 * g)
                    inc(e.activation(vstage[c], PS[:, 3 * ((g + 1) % 2) + c, 0:KVE], ACT.Copy), a_ev)
                    ge(e, a_ev, b * A_EV + n + 1)
                    dst = v_rows[bass.ds(b * KV, KV), t * P:(t + 1) * P, :].rearrange("h s d -> s h d")
                    inc(e.dma_start(dst, vstage[c].rearrange("p (h d) -> p h d", d=HD)), a_vst[c], 16)
                if not last:
                    a_hi(e, b + 1, DK - 1)

            for k in range(DK):
                a_hi(e, 0, k)
            p0_act_stored(e)
            with e.Fori(0, B - 1) as b:
                body(b, False)
            body(B - 1, True)

        def a_dve(e):
            for k in range(DK):
                a_lo(e, 0, k)
            with e.Fori(1, B) as b:
                a_norm(e, b)
                for k in range(DK):
                    a_lo(e, b, k)

        def a_stored(e):
            for c in range(3):
                ge(e, a_st[c], 16 * B * len(A_GROUPS))
            for t in range(2):
                ge(e, a_vst[t], 16 * B * (ST // 2))

        WO0 = 6
        wo_v = wo.rearrange("(i p) e -> p i e", p=P)
        wb_sp, wb_pe, wb_act, wb_dve, wb_lo, wb_tr = weight_prep(
            "wo", QC, lambda j: wo_v[:, :, bass.ds(j * P, P)], WO0, SF[:, 0:4 * D], nb=4)

        NG = B * KV
        NH = NG * G
        KB, VB, PB, QB = 0, 4 * T, 4608, Z0
        VW = HD
        kp = [[mmf(KB + p * 2 * T + i * T, T, HD) for i in range(2)] for p in range(2)]
        vp = [[mmf(VB + (2 * p + i) * NT * VW, NT * VW).rearrange("p (j d) -> p j d", j=NT) for i in range(2)] for p in range(2)]
        qp = [[mmf(QB + (2 * (1 - p) + i) * G * S, G * S, HD) for i in range(2)] for p in range(2)]
        pt = [[mmf(PB + (2 * j + i) * S, S) for i in range(2)] for j in range(NT)]
        assert VB + 4 * NT * VW <= PB and PB + 2 * NT * S <= WO0 * SLOT
        pu = [[SF[:, (hp * ST + u) * T:(hp * ST + u + 1) * T] for u in range(ST)] for hp in range(2)]
        OS0 = 2 * ST * T
        os_ = [SF[0:HD, OS0 + r * S:OS0 + (r + 1) * S] for r in range(2)]
        TH = T // 2
        su = [PS[:, 2 * i:2 * i + 2, :].rearrange("p b n -> p (b n)")[:, NB - TH:NB + TH] for i in range(2)]
        TB = [4, 5, 6, 4, 5]
        b_ld = [sem(f"b_loaded{p}") for p in range(2)]
        b_sp, b_S, b_T = sem("b_split"), sem("b_scores"), sem("b_transposed", 10)
        b_mx, b_ex, b_hi, b_lo = sem("b_max"), sem("b_exp", 2), sem("b_hi"), sem("b_lo", 5)
        b_pv, b_oe = sem("b_pv", 4), sem("b_o_left", 1)
        b_rc, b_nm, b_np = sem("b_recip"), sem("b_scaled"), sem("b_scaled_by_pool")
        b_os = [sem(f"b_o_stored{r}", 16) for r in range(2)]

        def b_loads(e, g, p):
            q = [
                e.dma_start(raw(kp[p][1]), k_d[bass.ds(g * HD, HD), :]),
                e.dma_start(raw(qp[p][1]).rearrange("p (h s) -> p h s", h=G),
                            q_d[bass.ds(g * (G * HD), G * HD), :].rearrange("(h p) s -> p h s", p=HD)),
                e.dma_start(raw(vp[p][1])[:, 0:ST, 0:HD], v_d[bass.ds(g * T, S), :].rearrange("(j p) d -> p j d", p=P)),
                e.dma_start(raw(vp[p][1])[0:C, ST, 0:HD], v_d[bass.ds(g * T + S, C), :]),
            ]
            for d in q:
                inc(d, b_ld[p], 16)

        def b_sp_eng(e):
            def body(i, last):
                for hh in range(2 * G):
                    n = i * (2 * G) + hh
                    p, a, r = hh // G, hh % G, hh % 2
                    if a == 0 and not (last and p == 1):
                        g = i * 2 + p
                        hold(e, b_pv, g * G)
                        b_loads(e, g + 1, 1 - p)
                    hold(e, b_oe, n + 1)
                    inc(e.dma_start(o_d[bass.ds(n * HD, HD), :], os_[r]), b_os[r], 16)
                    if last and hh == G - 1:
                        c_first_loads(e)

            with e.Fori(0, NG // 2 - 1) as i:
                body(i, False)
            body(NG // 2 - 1, True)

        PIECES = [[], ["k", "q0"], ["v", "q1"], ["q2", "q3"]]
        FIRST = ["k", "q0", "v", "q1", "q2", "q3"]

        def piece(nm, p):
            if nm == "k":
                return [(kp[p][0], kp[p][1])]
            if nm == "v":
                return [(vp[p][0][:, 0:ST, 0:HD], vp[p][1][:, 0:ST, 0:HD]), (vp[p][0][0:C, ST, 0:HD], vp[p][1][0:C, ST, 0:HD])]
            a = int(nm[1])
            return [tuple(t[:, a * S:(a + 1) * S] for t in qp[p])]

        def piece_hi(e, nm, p):
            for hi, lo in piece(nm, p):
                m = e.activation(hi, raw(lo), ACT.Copy)
            inc(m, b_ph)

        def piece_lo(e, nm, p, k):
            ge(e, b_ph, k + 1)
            for hi, lo in piece(nm, p):
                m = e.tensor_tensor(lo, raw(lo), raw(hi), ALU.subtract)
            inc(m, b_sp)

        def b_first_hi(e):
            ge(e, b_ld[0], 64)
            for nm in FIRST[:2]:
                piece_hi(e, nm, 0)

        def b_pool(e):
            def norm(m, mp, u):
                c = slice(mp * ST + u, mp * ST + u + 1)
                hold(e, b_rc, m * ST + u + 1)
                inc(e.tensor_scalar(pu[mp][u], pu[mp][u], rrec[:, c], None, ALU.mult), b_np)

            for k, nm in enumerate(FIRST):
                piece_lo(e, nm, 0, k)

            def body(i, last):
                for hh in range(2 * G):
                    n = i * (2 * G) + hh
                    p, a = hh // G, hh % G
                    nx = not (last and hh == 2 * G - 1)
                    todo = [] if last and p == 1 else PIECES[a]
                    done = (i * 2 + p + 1) * 6 + sum(len(q) for q in PIECES[:a])
                    for u in range(2 if nx else 0):
                        norm(n + 1, (hh + 1) % 2, u)
                    for k, nm in enumerate(todo):
                        piece_lo(e, nm, 1 - p, done + k)

            with e.Fori(0, NG // 2 - 1) as i:
                body(i, False)
            body(NG // 2 - 1, True)

        b_ph = sem("b_pool_hi")

        def b_pe(e):
            def scores(m, p, a, u):
                if u == 0:
                    ge(e, b_sp, six(m, a) + [2, 4, 5, 6][a])
                ge(e, b_ex, m * ST + u - 1)
                qh, ql = (t[:, a * S + u * P:a * S + (u + 1) * P] for t in qp[p])
                parts3(e, su[u % 2][:, 0:TH], qh, ql, kp[p][0][:, 0:TH], kp[p][1][:, 0:TH], True, True)
                inc(parts3(e, su[u % 2][:, TH:T], qh, ql, kp[p][0][:, TH:T], kp[p][1][:, TH:T], True, True), b_S)

            def transp(n, hp, j):
                if j == 0:
                    ge(e, b_np, n * 2 + 2)
                    ge(e, b_nm, n * 2 + 2)
                if j != 2:
                    wait = hold if j == ST else ge
                    wait(e, b_lo, n * NT + [-1, 0, 0, 1, 2][j])
                w = P if j < ST else C
                for u in range(ST):
                    m = e.transpose(PS[0:w, TB[j], u * P:(u + 1) * P], pu[hp][u][:, j * P:j * P + w], ident[:])
                inc(m, b_T)

            def pv(n, p, a, j):
                if j == 0:
                    ge(e, b_oe, n)
                    if a == 0:
                        ge(e, b_sp, six(n, a) + 3)
                ge(e, b_lo, n * NT + j + 1)
                w = P if j < ST else C
                vh, vl = (t[0:w, j, :] for t in vp[p])
                ph, pl = (t[0:w, :] for t in pt[j])
                m = parts3(e, PS[0:HD, 7, :], vh, vl, ph, pl, j == 0, j == NT - 1)
                if j == NT - 1:
                    inc(m, b_pv)

            cur = [0, 0]

            def six(m, a):
                return cur[1]

            def body(i, last):
                for hh in range(2 * G):
                    n = i * (2 * G) + hh
                    p, a = hh // G, hh % G
                    nx = None if (last and hh == 2 * G - 1) else n + 1
                    pn, an = ((hh + 1) // G) % 2, (hh + 1) % G
                    gn = i * 2 + (hh + 1) // G

                    def s(u):
                        if nx is not None:
                            cur[1] = gn * 6
                            scores(nx, pn, an, u)

                    def v(j):
                        cur[1] = (i * 2 + p) * 6
                        pv(n, p, a, j)

                    hp = hh % 2
                    for step in ("s0", "t0", "s1", "t1", "t2", "s2", "t3", "v0", "t4", "s3", "v1", "v2", "v3", "v4"):
                        q = int(step[1])
                        {"t": lambda: transp(n, hp, q), "s": lambda: s(q), "v": lambda: v(q)}[step[0]]()

            ge(e, wb_lo, QC)
            cur[1] = 0
            for u in range(ST):
                scores(0, 0, 0, u)
            with e.Fori(0, NG // 2 - 1) as i:
                body(i, False)
            body(NG // 2 - 1, True)

        def b_act(e):
            def exps(m, mp, u):
                if u == 0:
                    ge(e, b_T, (m - 1) * NT)
                ge(e, b_mx, m * ST + u + 1)
                inc(e.activation(pu[mp][u], su[u % 2][:, 0:T], ACT.Exp, bias=negmax[:, mp * ST + u:mp * ST + u + 1],
                                 accum_out=rsum[:, mp * ST + u:mp * ST + u + 1]), b_ex)

            def hi(n, j):
                ge(e, b_T, n * NT + j + 1)
                if j == 0:
                    ge(e, b_pv, n)
                w = P if j < ST else C
                inc(e.activation(pt[j][0][0:w, :], PS[0:w, TB[j], :], ACT.Copy), b_hi)

            def body(i, last):
                for hh in range(2 * G):
                    n = i * (2 * G) + hh
                    r = hh % 2
                    p, a = hh // G, hh % G
                    nx = not (last and hh == 2 * G - 1)
                    todo = [] if last and p == 1 else PIECES[a]
                    for step in ("h0", "e0", "h1", "h2", "e1", "h3", "c0", "h4", "e2", "e3"):
                        q = int(step[1])
                        if step[0] == "h":
                            hi(n, q)
                        elif step[0] == "e" and nx:
                            exps(n + 1, (hh + 1) % 2, q)
                        elif step[0] == "c" and todo:
                            if a == 1:
                                ge(e, b_ld[1 - p], (i + 1 + p) * 64)
                            piece_hi(e, todo[0], 1 - p)
                    ge(e, b_pv, n + 1)
                    ge(e, b_os[r], i * (16 * G) + 16 * (hh // 2))
                    inc(e.activation(os_[r], PS[0:HD, 7, :], ACT.Copy), b_oe)
                    for nm in todo[1:]:
                        piece_hi(e, nm, 1 - p)

            for u in range(ST):
                exps(0, 0, u)
                piece_hi(e, FIRST[2 + u], 0)
            with e.Fori(0, NG // 2 - 1) as i:
                body(i, False)
            body(NG // 2 - 1, True)

        def b_dve(e):
            def mx(m, mp, u):
                ge(e, b_S, m * ST + u + 1)
                inc(e.tensor_reduce(negmax[:, mp * ST + u:mp * ST + u + 1], su[u % 2][:, 0:T], AX.X, ALU.max, negate=True), b_mx)

            def recip(m, mp, u):
                c = slice(mp * ST + u, mp * ST + u + 1)
                ge(e, b_ex, m * ST + u + 1)
                inc(e.reciprocal(rrec[:, c], rsum[:, c]), b_rc)

            def norm(m, mp, u):
                c = slice(mp * ST + u, mp * ST + u + 1)
                ge(e, b_rc, m * ST + u + 1)
                inc(e.tensor_scalar(pu[mp][u], pu[mp][u], rrec[:, c], None, ALU.mult), b_np if u < 2 else b_nm)

            def lo(n, j):
                ge(e, b_hi, n * NT + j + 1)
                w = P if j < ST else C
                inc(e.tensor_tensor(pt[j][1][0:w, :], PS[0:w, TB[j], :], raw(pt[j][0][0:w, :]), ALU.subtract), b_lo)

            def body(i, last):
                for hh in range(2 * G):
                    n = i * (2 * G) + hh
                    nx = not (last and hh == 2 * G - 1)
                    mp = (hh + 1) % 2
                    for step in ("m0", "l0", "m1", "l1", "r0", "l2", "m2", "r1", "l3", "m3", "l4", "r2", "n2", "r3", "n3"):
                        q = int(step[1])
                        if step[0] == "l":
                            lo(n, q)
                        elif nx:
                            {"m": mx, "r": recip, "n": norm}[step[0]](n + 1, mp, q)

            for u in range(ST):
                mx(0, 0, u)
                recip(0, 0, u)
                norm(0, 0, u)
            with e.Fori(0, NG // 2 - 1) as i:
                body(i, False)
            body(NG // 2 - 1, True)

        halves = [SF[:, h * NB:(h + 1) * NB] for h in range(2)]
        j_ld = [sem(f"job_raw{h}") for h in range(2)]
        j_hi, j_lo = sem("job_hi"), sem("job_lo", 2)
        up_v = up_w.rearrange("(k p) n -> p k n", p=P)
        fc_v = fc1_w.rearrange("(k p) n -> p k n", p=P)

        def job_src(j, h):
            kind, c = j
            if kind == "e":
                w, c = (down_w, c) if c < FC else (w_d, c - FC)
                return w[c * P:(c + 1) * P, h * NB:(h + 1) * NB]
            return (up_v if kind == "u" else fc_v)[:, h * (DK // 2):(h + 1) * (DK // 2), c * P:(c + 1) * P]

        def job_slot(j):
            return FC + j[1] % 2 if j[0] == "f" else j[1]

        def job_load(e, j, m):
            for h in range(2):
                src = job_src(j, h)
                hold(e, j_lo, m * 2 + h - 1)
                o = halves[h] if len(src.shape) == 2 else halves[h].rearrange("p (k e) -> p k e", k=DK // 2)
                inc(e.dma_start(o, src), j_ld[h], 16)

        def job_part(j, h, part):
            return part(job_slot(j))[:, h * NB:(h + 1) * NB]

        def job_hi(e, j, m, free=None):
            if free:
                free()
            for h in range(2):
                ge(e, j_ld[h], m * 16 + 16)
                inc(e.activation(job_part(j, h, slot_hi), halves[h], ACT.Copy), j_hi)

        def job_lo(e, j, m, done):
            for h in range(2):
                ge(e, j_hi, m * 2 + h + 1)
                inc(e.tensor_tensor(job_part(j, h, slot_lo), halves[h], raw(job_part(j, h, slot_hi)), ALU.subtract), j_lo)
            ge(e, j_lo, m * 2 + 2)
            e.sem_inc(sems[done][0], 1)

        D_GROUPS = [[("u", 0), ("u", 1), ("u", 2)], [("u", 3), ("u", 4), ("u", 5)], [("f", 0), ("u", 6), ("u", 7)],
                    [("f", 1), ("u", 8), ("u", 9)], [("f", 2), ("u", 10), ("u", 11)], [("u", 12), ("u", 13)],
                    [("f", 3), ("u", 14), ("u", 15)]]
        JOBS_C = {0: [("u", 0)], 1: [("u", 1), ("u", 2)], 2: [("u", 3), ("u", 4)]}
        JOBS_FIRST = {-1: [("u", 5)] + D_GROUPS[2], 0: D_GROUPS[3], 1: [("u", 10), ("u", 11)], 2: [("f", 2), ("u", 12), ("u", 13)],
                      3: D_GROUPS[6], 4: [("f", 0)]}
        JOBS_MID = {-1: [("f", 1)], 2: [("f", 2)], 3: [("f", 3)], 4: [("f", 0)]}
        JOBS_LAST = {-1: [("f", 1)], 0: [("e", 0), ("e", 1), ("e", 2)], 1: [("e", 3), ("e", 4), ("e", 5)],
                     2: [("f", 2), ("e", 6), ("e", 7)], 3: [("f", 3), ("e", 8), ("e", 9)], 4: [("e", 10), ("e", 11)],
                     5: [("e", 12), ("e", 13)]}
        JOBS_E = [("e", c) for c in range(14, FC + LC)]

        def flat(jobs):
            return [(at, j) for at in sorted(jobs) for j in jobs[at]]

        N_C = len(flat(JOBS_C))
        N_FIRST = len(flat(JOBS_FIRST))
        N_MID = len(flat(JOBS_MID))
        N_LAST = len(flat(JOBS_LAST))
        M_FIRST = N_C
        M_MID = M_FIRST + N_FIRST
        M_LAST = M_MID + N_MID * (B - 2)
        M_E = M_LAST + N_LAST
        d_up, d_fc, e_sl = sem("d_up_slots"), sem("d_fc_slots"), sem("e_slots")
        DONE = {"u": d_up, "f": d_fc, "e": e_sl}

        CU = QC // 4
        CUB = Z0 + 2 * DK * S - 8 * CU * P
        cu = [[mmf(CUB + (2 * u + i) * CU * P, CU * P).rearrange("p (c s) -> p c s", c=CU) for i in range(2)] for u in range(4)]
        assert CUB >= QB + 2 * G * S
        XR = SF[:, 5 * D:6 * D]
        XN2 = SF[:, D:D + ST * D].rearrange("p (t d) -> p t d", t=ST)
        cc_ld = [sem(f"c_o_loaded{u}") for u in range(4)]
        cc_xl = sem("c_x_loaded")
        cc_hi, cc_lo = sem("c_o_hi"), sem("c_o_lo")
        cc_use, cc_x1 = sem("c_unit_used", 4), sem("c_x1", 2)
        cc_st = sem("c_stored")
        d_acc = sem("d_product", 20)

        d_load, d_norm, d_sqrt, d_pet0, d_hi, d_lo, d_zl, d_fr, d_zt = norm_z(
            "d", XN2, lambda e, b: ge(e, d_acc, b * ND))

        def c_load_unit(e, b, t, u):
            n = b * ST + t
            hold(e, cc_use, n * 4 + u - 3)
            src = o_d[bass.ds(b * E + u * CU * P, CU * P), t * P:(t + 1) * P]
            inc(e.dma_start(raw(cu[u][1]), src.rearrange("(c p) s -> p c s", p=P)), cc_ld[u], 16)

        def c_first_loads(e):
            hold(e, b_pv, (NG - 1) * G)
            for r in range(2):
                ge(e, b_os[r], H // 2 * 16)
            for u in range(4):
                c_load_unit(e, 0, 0, u)

        def c_sp_eng(e):
            def load_x(n):
                inc(e.dma_start(XR, x_r[bass.ds(n * P, P), :]), cc_xl, 16)

            def tiles(b, t0, jobs=None):
                m = 0
                for r in range(2):
                    hold(e, b_os[r], b * (H // 2 * 16) + H // 2 * 16)
                for t in range(t0, ST):
                    n = b * ST + t
                    for u in range(4):
                        c_load_unit(e, b, t, u)
                    hold(e, cc_x1, n)
                    inc(e.dma_start(x1_d[bass.ds(n * P - P, P), :], XR), cc_st, 16)
                    hold(e, cc_st, n * 16)
                    load_x(n)
                    for j in (jobs or {}).get(t, []):
                        job_load(e, j, m)
                        m += 1
                    if jobs and t == 0:
                        d_load(e, x1_d, 0)

            hold(e, b_pv, NH)
            for r in range(2):
                ge(e, b_os[r], NH // 2 * 16)
            load_x(0)
            tiles(0, 1)
            with e.Fori(1, B - 1) as b:
                tiles(b, 0)
            tiles(B - 1, 0, JOBS_C)
            hold(e, cc_x1, B * ST)
            inc(e.dma_start(x1_d[(B * ST - 1) * P:B * ST * P, :], XR), cc_st, 16)
            ge(e, cc_st, B * ST * 16)

        def c_act(e):
            def tiles(b, jobs=None):
                m = 0
                for t in range(ST):
                    n = b * ST + t
                    for u in range(4):
                        ge(e, cc_ld[u], n * 16 + 16)
                        inc(e.activation(cu[u][0], raw(cu[u][1]), ACT.Copy), cc_hi)
                    if jobs and t == 1:
                        d_sqrt(e, 0)
                    for j in (jobs or {}).get(t, []):
                        job_hi(e, j, m)
                        m += 1

            with e.Fori(0, B - 1) as b:
                tiles(b)
            tiles(B - 1, JOBS_C)
            for k in range(DK):
                d_hi(e, 0, k)

        def c_pool(e):
            def tiles(b, jobs=None):
                m = 0
                for t in range(ST):
                    n = b * ST + t
                    for u in range(4):
                        ge(e, cc_hi, n * 4 + u + 1)
                        inc(e.tensor_tensor(cu[u][1], raw(cu[u][1]), raw(cu[u][0]), ALU.subtract), cc_lo)
                    for j in (jobs or {}).get(t, []):
                        job_lo(e, j, m, DONE[j[0]])
                        m += 1

            with e.Fori(0, B - 1) as b:
                tiles(b)
            tiles(B - 1, JOBS_C)

        def units_under(k):
            over = Z0 + DK * S + (k + 1) * S - CUB
            return 0 if over <= 0 else -(-over // (2 * CU * P))

        def c_pe(e):
            at = {0: [0, 1], 2: [2], 4: [3], 8: [4], 9: [5], 11: [6]}

            def tile(b, t, transposes=False):
                n = b * ST + t
                ge(e, cc_x1, n - 1)
                for k in range(QC):
                    u, c = k // CU, k % CU
                    if transposes:
                        for q in at.get(k, []):
                            d_pet0(e, 0, q)
                    if c == 0:
                        ge(e, cc_lo, n * 4 + u + 1)
                    wh, wl = slot_hi(WO0 + k), slot_lo(WO0 + k)
                    for h in range(2):
                        hs = slice(h * NB, (h + 1) * NB)
                        m = parts3(e, PS[:, 2 * (t % 2) + h, :], cu[u][0][:, c, :], cu[u][1][:, c, :],
                                   wh[:, hs], wl[:, hs], k == 0, k == QC - 1)
                    if c == CU - 1:
                        inc(m, cc_use)

            ge(e, b_ex, NH * ST)
            with e.Fori(0, B - 1) as b:
                for t in range(ST):
                    tile(b, t)
            for t in range(ST):
                tile(B - 1, t, t == ST - 1)
            d_pet0(e, 0, DK - 1)

        def c_dve(e):
            def tile(b, t):
                n, r = b * ST + t, t % 2
                ge(e, cc_use, n * 4 + 4)
                ge(e, cc_xl, n * 16 + 16)
                inc(e.tensor_tensor(XR, PS[:, 2 * r:2 * r + 2, :].rearrange("p b n -> p (b n)"), XR, ALU.add), cc_x1)

            with e.Fori(0, B - 1) as b:
                for t in range(ST):
                    tile(b, t)
            for t in range(ST - 1):
                tile(B - 1, t)
                if t == 0:
                    d_norm(e, 0)
            for k in range(DK):
                if k == DK - 2:
                    tile(B - 1, ST - 1)
                if units_under(k):
                    ge(e, cc_use, (B * ST - 1) * 4 + units_under(k))
                d_lo(e, 0, k)

        st2 = [SF[:, 5 * D + c * NB:5 * D + (c + 1) * NB] for c in range(3)]
        D_ALL = [c for g in D_GROUPS for c in g]
        D_CUM = [sum(len(x) for x in D_GROUPS[:g + 1]) for g in range(len(D_GROUPS))]
        ND = len(D_ALL)
        assert ND == FC + LC == 20 and FC == 16 and LC == 4
        d_ev, d_sq = sem("d_staged", 3), sem("d_squared")
        d_st = [sem(f"d_stored{c}", 16) for c in range(3)]
        D_USES = [sum(len(x) > c for x in D_GROUPS) for c in range(3)]
        d_gm, d_gc = sem("d_gate_product"), sem("d_gate_chain", 1)
        d_gw = sem("d_gate_weights")
        d_gl, d_gt = sem("d_gate_staged"), sem("d_gate_transposed")
        gTs = sm[:, 216:216 + P]
        gT = [gTs[32 * t:32 * t + 2 * NE, :] for t in range(ST)]
        GC = 7

        def jobs_of(b):
            if isinstance(b, int):
                return (JOBS_FIRST, M_FIRST) if b == 0 else (JOBS_LAST, M_LAST)
            return JOBS_MID, b * N_MID + (M_MID - N_MID)

        def d_sp_eng(e):
            for b in (0, None, B - 1):
                def run(b, n_before):
                    for m, (at, j) in enumerate(flat(jobs_of(b)[0])):
                        job_load(e, j, n_before + m)

                if b is not None:
                    run(b, jobs_of(b)[1])
                else:
                    with e.Fori(1, B - 1) as r:
                        run(r, jobs_of(r)[1])

        def d_pool(e):
            for b in (0, None, B - 1):
                def run(b, n_before):
                    for m, (at, j) in enumerate(flat(jobs_of(b)[0])):
                        job_lo(e, j, n_before + m, DONE[j[0]])

                if b is not None:
                    run(b, jobs_of(b)[1])
                else:
                    with e.Fori(1, B - 1) as r:
                        run(r, jobs_of(r)[1])

        def d_pe(e):
            def pet(e, b, k):
                if k == 0:
                    ge(e, d_gc, b * GC)
                d_pet0(e, b, k)

            def body(b, last):
                def wait_bank(g, c):
                    if g == 0:
                        ge(e, d_ev, b * ND - 2 + c)
                    elif c == 0:
                        ge(e, d_ev, b * ND + (D_CUM[g - 2] if g >= 2 else 0))

                def slot_ready(ch):
                    if ch[0] == "u":
                        ge(e, d_up, ch[1] + 1)
                    else:
                        ge(e, d_fc, b * LC + ch[1] + 1)

                def gate(g):
                    if g == 0:
                        ge(e, d_gw, 18)
                        for k in range(DK):
                            e.matmul(PS[0:2 * NE, 6, :], GW[:, k, :], zhi[:, k, :], start=k == 0, stop=False)
                            m = e.matmul(PS[0:2 * NE, 6, :], GW[:, k, :], zlo[:, k, :], start=False, stop=k == DK - 1)
                        inc(m, d_gm)
                    if g == 1:
                        hold(e, d_gl, b + 1)
                        inc(e.transpose(PS[:, 6, 0:P], gTs, ident[:]), d_gt)

                mm_groups(e, b, D_GROUPS, d_zl, wait_bank, job_slot, d_acc, slot_ready, gate, d_fr, None if last else pet)

            ge(e, cc_x1, B * ST)
            with e.Fori(0, B - 1) as b:
                body(b, False)
            body(B - 1, True)

        def d_act(e):
            def body(b, last):
                jobs, m0 = jobs_of(b)
                m = [0]

                def run(at, b):
                    for j in jobs.get(at, []):
                        done_before = {("f", 0): (0, 4), ("f", 1): (-1, 6), ("f", 2): (0, 2), ("f", 3): (0, 3)}
                        free = None
                        if j[0] == "e":
                            free = lambda: ge(e, d_acc, b * ND + D_ALL.index(("u", j[1])) + 1)
                        elif j[0] == "f" and not (isinstance(b, int) and b == 0 and at <= 0):
                            db, g = done_before[j]
                            free = lambda: ge(e, d_acc, (b + db) * ND + D_CUM[g])
                        elif at == -1:
                            free = lambda: ge(e, cc_use, B * ST * 4)
                        job_hi(e, j, m0 + m[0], free)
                        m[0] += 1

                run(-1, b)
                n, sq = 0, 0
                for g, chunks in enumerate(D_GROUPS):
                    if g == len(D_GROUPS) - 1 and not last:
                        for k in range(DK - 1):
                            d_hi(e, b + 1, k)
                    for c, ch in enumerate(chunks):
                        ge(e, d_acc, b * ND + n + c + 1)
                        ge(e, d_st[c], b * (16 * D_USES[c]) + 16 * sum(len(x) > c for x in D_GROUPS[:g]))
                        inc(e.activation(st2[c], PS[:, 3 * (g % 2) + c, :], ACT.Relu if ch[0] == "u" else ACT.Copy), d_ev)
                    if g == len(D_GROUPS) - 1 and not last:
                        d_hi(e, b + 1, DK - 1)
                    for c, ch in enumerate(chunks):
                        up = ch[0] == "u"
                        if up:
                            sq += 1
                            ge(e, d_sq, b * FC + sq)
                        else:
                            ge(e, d_ev, b * ND + n + 1)
                        row = ch[1] * P if up else F + ch[1] * P
                        inc(e.dma_start(h_d[bass.ds(b * (F + L) + row, P), :], st2[c]), d_st[c], 16)
                        n += 1
                    run(g, b)
                    if g == 0 and not last:
                        d_load(e, x1_d, b + 1)
                    if g == 2 and not last:
                        d_sqrt(e, b + 1)

            body(0, False)
            with e.Fori(1, B - 1) as b:
                body(b, False)
            body(B - 1, True)

        def d_dve(e):
            def body(b, last):
                n = 0
                for g, chunks in enumerate(D_GROUPS):
                    final = g == len(D_GROUPS) - 1 and not last
                    for k in range(DK - 1 if final else 0):
                        d_lo(e, b + 1, k)
                    for c, ch in enumerate(chunks):
                        if ch[0] == "u":
                            ge(e, d_ev, b * ND + n + 1)
                            inc(e.tensor_tensor(st2[c], st2[c], st2[c], ALU.mult), d_sq)
                        n += 1
                    if final:
                        d_lo(e, b + 1, DK - 1)
                    if g == 0:
                        hold(e, d_gm, b + 1)
                        for t in range(ST):
                            m = e.tensor_copy(gT[t], PS[0:2 * NE, 6, t * P:(t + 1) * P])
                        inc(m, d_gl)
                    if g == 1:
                        hold(e, d_gt, b + 1)
                        q = [0]

                        def link(ins):
                            q[0] += 1
                            inc(ins, d_gc)
                            hold(e, d_gc, b * GC + q[0])

                        link(e.tensor_copy(gsum, PS[:, 6, 0:P].rearrange("p (t e) -> p t e", t=ST)[:, :, 0:2 * NE]))
                        link(e.tensor_tensor(g8, gsum[:, :, 0:NE], gsum[:, :, NE:2 * NE], ALU.add))
                        for t in range(ST):
                            link(e.max(gtop[:, t, :], g8[:, t, :]))
                        link(e.tensor_tensor(rw[:, bass.ds(b * ST, ST)], gtop[:, :, 0], gtop[:, :, 1], ALU.add))
                        assert q[0] == GC
                    if g == 2 and not last:
                        d_norm(e, b + 1)

            ge(e, d_gw, 16)
            inc(e.tensor_copy(GW[:, :, 0:NE], graw), d_gw)
            ge(e, d_gw, 17)
            inc(e.tensor_tensor(GW[:, :, NE:2 * NE], graw, raw(GW[:, :, 0:NE]), ALU.subtract), d_gw)
            ge(e, d_gw, 18)
            inc(e.memset(gTs, 0.0), d_gw)
            ge(e, d_gw, 19)
            with e.Fori(0, B - 1) as b:
                body(b, False)
            body(B - 1, True)

        NK = FC + LC
        EU = NK // 4
        H0 = NK * SLOT
        eu = [[mmf(H0 + (2 * u + i) * EU * P, EU * P).rearrange("p (c s) -> p c s", c=EU) for i in range(2)] for u in range(4)]
        x1b = SF[:, D:2 * D]
        yb = [SF[:, (2 + r) * D:(3 + r) * D] for r in range(2)]
        gam, bet = SF[:, 4 * D:5 * D], SF[:, 5 * D:6 * D]
        e_ld = [sem(f"e_h_loaded{u}") for u in range(4)]
        e_hi, e_lo, e_use = sem("e_h_hi"), sem("e_h_lo"), sem("e_unit_used", 4)
        e_y, e_add, e_sq, e_ch = sem("e_routed"), sem("e_added", 2), sem("e_sqrt"), sem("e_chain")
        e_post = sem("e_post", 1)
        e_gb, e_xl = sem("e_gamma_beta"), sem("e_x1_loaded")
        e_st = [sem(f"e_stored{r}", 16) for r in range(2)]
        E_CHAIN = 12

        def e_load(e, b, t, u):
            n = b * ST + t
            hold(e, e_use, n * 4 + u - 3)
            src = h_d[bass.ds(b * (F + L) + u * EU * P, EU * P), t * P:(t + 1) * P]
            inc(e.dma_start(raw(eu[u][1]), src.rearrange("(c p) s -> p c s", p=P)), e_ld[u], 16)

        def e_load_x1(e, n):
            hold(e, e_post, n)
            inc(e.dma_start(x1b, x1_d[bass.ds(n * P, P), :]), e_xl, 16)

        def e_sp_eng(e):
            for c in range(3):
                ge(e, d_st[c], 16 * D_USES[c])
            job_load(e, JOBS_E[0], M_E)
            hold(e, d_acc, B * ND)
            for u in range(4):
                e_load(e, 0, 0, u)
            for c in range(3):
                ge(e, d_st[c], B * (16 * D_USES[c]))
            for m, j in enumerate(JOBS_E[1:], 1):
                job_load(e, j, M_E + m)
            inc(e.dma_start(gam, gamma.partition_broadcast(P)), e_gb, 16)
            inc(e.dma_start(bet, beta.partition_broadcast(P)), e_gb, 16)
            e_load_x1(e, 0)

            def rest(b, t0):
                for t in range(t0, ST):
                    for u in range(4):
                        e_load(e, b, t, u)
                    e_load_x1(e, b * ST + t)

            rest(0, 1)
            with e.Fori(1, B) as b:
                rest(b, 0)

        def e_pool(e):
            def split(n, u):
                ge(e, e_hi, n * 4 + u + 1)
                inc(e.tensor_tensor(eu[u][1], raw(eu[u][1]), raw(eu[u][0]), ALU.subtract), e_lo)

            for u in range(4):
                split(0, u)
            for t in range(1, ST):
                for u in range(4):
                    split(t, u)
            with e.Fori(1, B) as b:
                for t in range(ST):
                    for u in range(4):
                        split(b * ST + t, u)

        def e_pe(e):
            ge(e, d_ev, B * ND)
            ge(e, d_gc, B * GC)
            with e.Fori(0, B) as b:
                for t in range(ST):
                    n = b * ST + t
                    ge(e, e_add, n - 1)
                    for k in range(NK):
                        u, c = k // EU, k % EU
                        if c == 0:
                            ge(e, e_lo, n * 4 + u + 1)
                        if t == 0:
                            ge(e, e_sl, k + 1)
                        wh, wl = slot_hi(k), slot_lo(k)
                        for h in range(2):
                            hs = slice(h * NB, (h + 1) * NB)
                            bank = 4 * (t % 2) + (0 if k < FC else 2) + h
                            m = parts3(e, PS[:, bank, :], eu[u][0][:, c, :], eu[u][1][:, c, :],
                                       wh[:, hs], wl[:, hs], k in (0, FC), k in (FC - 1, NK - 1))
                        if c == EU - 1:
                            inc(m, e_use)

        def bank2(i):
            return PS[:, i:i + 2, :].rearrange("p b n -> p (b n)")

        def e_act(e):
            def hi(n, u):
                ge(e, e_ld[u], n * 16 + 16)
                inc(e.activation(eu[u][0], raw(eu[u][1]), ACT.Copy), e_hi)

            def step(b, t, more):
                n, r = b * ST + t, t % 2
                if more:
                    for u in range(3):
                        hi(n + 1, u)
                ge(e, e_use, n * 4 + 4)
                ge(e, e_st[r], b * (16 * ST // 2) + 16 * (t // 2))
                inc(e.activation(yb[r], bank2(4 * r + 2), ACT.Copy, scale=rw[:, bass.ds(n, 1)]), e_y)
                if more:
                    hi(n + 1, 3)
                ge(e, e_ch, n * E_CHAIN + 7)
                inc(e.activation(rt[:, 0:1], rec[:, 0:1], ACT.Sqrt), e_sq)
                ge(e, e_post, n + 1)
                inc(e.dma_start(out_r[bass.ds(n * P, P), :], yb[r]), e_st[r], 16)

            for u in range(4):
                hi(0, u)
            for m, j in enumerate(JOBS_E):
                job_hi(e, j, M_E + m)
            with e.Fori(0, B - 1) as b:
                for t in range(ST):
                    step(b, t, True)
            for t in range(ST):
                step(B - 1, t, t < ST - 1)
            for r in range(2):
                ge(e, e_st[r], B * (16 * ST // 2))

        def e_dve(e):
            for m, j in enumerate(JOBS_E):
                job_lo(e, j, M_E + m, e_sl)
            ge(e, e_gb, 32)
            with e.Fori(0, B) as b:
                for t in range(ST):
                    n, r = b * ST + t, t % 2
                    q = [0]

                    def link(ins, last=True):
                        q[0] += 1
                        inc(ins, e_ch)
                        if last:
                            hold(e, e_ch, n * E_CHAIN + q[0])

                    ge(e, e_xl, n * 16 + 16)
                    link(e.tensor_tensor(x1b, x1b, bet, ALU.add))
                    ge(e, e_y, n + 1)
                    inc(e.tensor_tensor(yb[r], bank2(4 * r), yb[r], ALU.add), e_add)
                    ge(e, e_add, n + 1)
                    for h in range(2):
                        link(e.bn_stats(stats[:, 0, h, :], yb[r][:, h * NB:(h + 1) * NB]), h == 1)
                    link(e.bn_aggr(mv[:, 0, :], stats[:, 0, :, :]))
                    link(e.tensor_scalar(ve[:, 0:1], mv[:, 0, 1:2], EPS, None, ALU.add))
                    link(e.reciprocal(rec[:, 0:1], ve[:, 0:1]))
                    link(e.tensor_scalar(rec[:, 1:2], ve[:, 0:1], -0.5, None, ALU.mult))
                    hold(e, e_sq, n + 1)
                    link(e.tensor_tensor(nt1[:, 0:1], rt[:, 0:1], rt[:, 0:1], ALU.mult))
                    link(e.tensor_tensor(nt1[:, 0:1], nt1[:, 0:1], rec[:, 1:2], ALU.mult))
                    link(e.tensor_scalar(nt1[:, 0:1], nt1[:, 0:1], 1.5, None, ALU.add))
                    link(e.tensor_tensor(rstd[:, 0:1], rt[:, 0:1], nt1[:, 0:1], ALU.mult))
                    link(e.scalar_tensor_tensor(yb[r], yb[r], mv[:, 0, 0:1], gam, ALU.subtract, ALU.mult))
                    assert q[0] == E_CHAIN
                    inc(e.scalar_tensor_tensor(yb[r], yb[r], rstd[:, 0:1], x1b, ALU.mult, ALU.add), e_post)

        block = es.enter_context(nc.Block())

        @block.sync
        def _(e):
            p0_sp(e)
            a_sp(e)
            hold(e, a_zt, B * DK)
            inc(e.dma_start(graw, gate_w.rearrange("(k p) e -> p k e", p=P)), d_gw, 16)
            wb_sp(e, 0, 2)
            a_stored(e)
            b_loads(e, 0, 0)
            wb_sp(e, 2)
            b_sp_eng(e)
            c_sp_eng(e)
            d_sp_eng(e)
            e_sp_eng(e)

        @block.gpsimd
        def _(e):
            for h, credit in sems.values():
                if credit:
                    e.sem_inc(h, credit)
            inc(e.memset(ident[:], 0.0), ph_start)
            ge(e, ph_start, 1)
            inc(e.affine_select(out=ident[:], in_=ident[:], compare_op=ALU.not_equal, fill=1.0, base=0,
                                pattern=[[-1, P]], channel_multiplier=1), ph_start)
            f_pool(e)
            b_pool(e)
            c_pool(e)
            d_pool(e)
            e_pool(e)

        @block.scalar
        def _(e):
            p0_act(e)
            a_act(e)
            wb_act(e, 0, 2)
            b_first_hi(e)
            wb_act(e, 2)
            b_act(e)
            c_act(e)
            d_act(e)
            e_act(e)

        @block.vector
        def _(e):
            p0_dve(e)
            a_dve(e)
            wb_dve(e)
            b_dve(e)
            c_dve(e)
            d_dve(e)
            e_dve(e)

        @block.tensor
        def _(e):
            p0_pe(e)
            a_pe(e)
            ge(e, a_ev, B * A_EV)
            wb_pe(e)
            b_pe(e)
            c_pe(e)
            d_pe(e)
            e_pe(e)


_P = "L0_xattn_"
_F = "L0_ffn_"


def kernel(**inputs):
    import numpy as np
    import concourse.bacc as bacc
    from concourse.bass_utils import run_bass_kernel_spmd

    arrays = {
        "x": inputs["x"],
        "ctx": inputs["ctx_4096"],
        "wqkv": np.concatenate([np.asarray(inputs[_P + w]) for w in ("Wq", "Wk", "Wv")], axis=0),
        "wo": inputs[_P + "Wo"],
        "gate_w": inputs[_F + "gate_w"],
        "up_w": inputs[_F + "up_w"],
        "down_w": inputs[_F + "down_w"],
        "fc1_w": inputs[_F + "fc1_w"],
        "fc2_w": inputs[_F + "fc2_w"],
        "expert_w": inputs[_F + "expert_w"],
        "gamma": inputs[_F + "ln_gamma"],
        "beta": inputs[_F + "ln_beta"],
    }
    arrays = {f"in_{k}": np.ascontiguousarray(v) for k, v in arrays.items()}
    nc = bacc.Bacc("TRN2", target_bir_lowering=False, num_devices=1)
    aps = [nc.dram_tensor(k, v.shape, mybir.dt.from_np(v.dtype), kind="ExternalInput").ap() for k, v in arrays.items()]
    out = nc.dram_tensor("out", arrays["in_x"].shape, mybir.dt.float32, kind="ExternalOutput").ap()
    xattn_ffn_kernel(nc, *aps, out)
    r = run_bass_kernel_spmd(nc, [arrays], core_ids=[0])
    return r.results[0]["out"]
```
